# Optimizing a Trainium2 kernel written in Bass

```python
import numpy as np
import jax
import jax.numpy as jnp

def _softmax(x, axis=-1):
    return jax.nn.softmax(x, axis=axis)

def _gelu(x):
    return jax.nn.gelu(x, approximate=True)

def _silu(x):
    return jax.nn.silu(x)

def _sigmoid(x):
    return jax.nn.sigmoid(x)

def _layernorm(x, axis=-1, eps=1e-05):
    m = jnp.mean(x, axis=axis, keepdims=True)
    v = jnp.var(x, axis=axis, keepdims=True)
    return (x - m) / jnp.sqrt(v + eps)

def _scatter_add(tgt, idx, src, axis=0):
    return tgt.at[idx].add(src)

def _segment_sum(src, seg, n):
    return jax.ops.segment_sum(src, seg, n)
kernel_name = 'mk_xattn_ffn_d1_seqx_r4_145707'

def setup_inputs(seed: int=0):
    np.random.seed(seed)
    _w = jnp.asarray

    def _rec_inputs():
        import jax
        import jax.numpy as jnp
        _rk = jax.random.key(seed)
        x = -7.109e-05 + 0.9999 * jax.random.normal(jax.random.fold_in(_rk, 1), (4, 512, 512), jnp.float32)
        _lenS = 512 - jax.random.randint(jax.random.fold_in(_rk, 7), (4,), 0, max(1, 512 // 4) + 1, jnp.int32)
        _lenS2 = 512 - jax.random.randint(jax.random.fold_in(_rk, 8), (4,), 0, max(1, 512 // 4) + 1, jnp.int32)
        _ctx_2048P = jax.random.normal(jax.random.fold_in(_rk, 11), (4, 16, 512), jnp.float32)
        _ctx_2048c = jax.random.dirichlet(jax.random.fold_in(_rk, 511), 0.3 * jnp.ones((16,), jnp.float32), (4, 512))
        _ctx_2048t = jnp.einsum('bsk,bkd->bsd', _ctx_2048c, _ctx_2048P)
        _ctx_2048t = _ctx_2048t * jax.lax.rsqrt(jnp.mean(jnp.square(_ctx_2048t)) + 1e-12) * 0.953939
        ctx_2048 = -3.05549e-07 + 0.0199987 * (_ctx_2048t + 0.3 * jax.random.normal(jax.random.fold_in(_rk, 611), (4, 512, 512), jnp.float32))
        return (x, ctx_2048)
    x, ctx_2048 = _rec_inputs()

    def _L0_xattn_setup():
        import jax, jax.numpy as jnp
        import numpy as np
        FP8_MAX = 448.0
        ACT_EPS = 0.0001
        W_EPS = 1e-06
        BLK = 128

        def quant_dequant_act_1x128(x):
            E, M, K = x.shape
            xb = x.reshape(E, M, K // BLK, BLK)
            amax = jnp.max(jnp.abs(xb), axis=-1, keepdims=True)
            safe = jnp.maximum(amax, ACT_EPS)
            q = (xb * (FP8_MAX / safe)).astype(jnp.float8_e4m3fn)
            return (q.astype(jnp.float32) * (safe / FP8_MAX)).reshape(E, M, K)

        def quant_dequant_weight_128x128(w):
            E, N, K = w.shape
            wb = w.reshape(E, N // BLK, BLK, K // BLK, BLK)
            amax = jnp.max(jnp.abs(wb), axis=(2, 4), keepdims=True)
            safe = jnp.maximum(amax, W_EPS)
            q = (wb * (FP8_MAX / safe)).astype(jnp.float8_e4m3fn)
            return (q.astype(jnp.float32) * (safe / FP8_MAX)).reshape(E, N, K)
        key = jax.random.key(seed)
        kx, kw = jax.random.split(key)
        E, M, K, N = (8, 1024, 512, 512)
        x = jax.random.normal(kx, (E, M, K), dtype=jnp.float32)
        weight = jax.random.normal(kw, (E, N, K), dtype=jnp.float32) * 0.02
        return {'x': x, 'weight': weight}
    _L0_xattn_all = _L0_xattn_setup()
    _L0_xattn_in = {k: v for k, v in _L0_xattn_all.items() if k in ()}
    del _L0_xattn_all

    def _L0_ffn_setup():
        import jax, jax.numpy as jnp
        import numpy as np
        ROPE_THETA = 1000000.0
        TOP_K = 2

        def rmsnorm(x, w, eps=1e-06):
            xf = x.astype(jnp.float32)
            n = jax.lax.rsqrt(jnp.mean(xf * xf, axis=-1, keepdims=True) + eps)
            return (xf * n).astype(x.dtype) * w

        def rope_tables(seq_len, head_dim):
            freqs = 1.0 / ROPE_THETA ** (jnp.arange(0, head_dim, 2, dtype=jnp.float32) / head_dim)
            t = jnp.arange(seq_len, dtype=jnp.float32)
            f = jnp.outer(t, freqs)
            return (jnp.cos(f), jnp.sin(f))

        def apply_rope(x, cos, sin):
            half = x.shape[-1] // 2
            x1, x2 = (x[..., :half], x[..., half:])
            c = cos[None, None]
            s = sin[None, None]
            return jnp.concatenate([x1 * c - x2 * s, x2 * c + x1 * s], axis=-1)
        key = jax.random.key(seed)
        ks = jax.random.split(key, 8)
        B, S, D = (2, 512, 512)
        Hq, Hkv, hd = (16, 4, 128)
        E, I = (8, 352)
        sc = 0.02
        return {'hidden': jax.random.normal(ks[0], (B, S, D), jnp.float32), 'attn_norm_w': jnp.ones((D,), jnp.float32), 'q_w': jax.random.normal(ks[1], (Hq * hd, D), jnp.float32) * sc, 'k_w': jax.random.normal(ks[2], (Hkv * hd, D), jnp.float32) * sc, 'v_w': jax.random.normal(ks[3], (Hkv * hd, D), jnp.float32) * sc, 'o_w': jax.random.normal(ks[4], (D, Hq * hd), jnp.float32) * sc, 'q_norm_w': jnp.ones((hd,), jnp.float32), 'k_norm_w': jnp.ones((hd,), jnp.float32), 'ffn_norm_w': jnp.ones((D,), jnp.float32), 'gate_w': jax.random.normal(ks[5], (E, D), jnp.float32) * sc, 'wg': jax.random.normal(ks[6], (E, I, D), jnp.float32) * sc, 'wu': jax.random.normal(ks[7], (E, I, D), jnp.float32) * sc, 'wd': jax.random.normal(jax.random.fold_in(key, 99), (E, D, I), jnp.float32) * sc}
    _L0_ffn_all = _L0_ffn_setup()
    _L0_ffn_in = {k: v for k, v in _L0_ffn_all.items() if k in ('attn_norm_w', 'q_w', 'k_w', 'v_w', 'o_w', 'q_norm_w', 'k_norm_w', 'ffn_norm_w', 'gate_w', 'wg', 'wu', 'wd')}
    del _L0_ffn_all
    return {'x': x, 'ctx_2048': ctx_2048, 'L0_ffn_attn_norm_w': _L0_ffn_in['attn_norm_w'], 'L0_ffn_q_w': _L0_ffn_in['q_w'], 'L0_ffn_k_w': _L0_ffn_in['k_w'], 'L0_ffn_v_w': _L0_ffn_in['v_w'], 'L0_ffn_o_w': _L0_ffn_in['o_w'], 'L0_ffn_q_norm_w': _L0_ffn_in['q_norm_w'], 'L0_ffn_k_norm_w': _L0_ffn_in['k_norm_w'], 'L0_ffn_ffn_norm_w': _L0_ffn_in['ffn_norm_w'], 'L0_ffn_gate_w': _L0_ffn_in['gate_w'], 'L0_ffn_wg': _L0_ffn_in['wg'], 'L0_ffn_wu': _L0_ffn_in['wu'], 'L0_ffn_wd': _L0_ffn_in['wd']}

def reference(x, ctx_2048, L0_ffn_attn_norm_w, L0_ffn_q_w, L0_ffn_k_w, L0_ffn_v_w, L0_ffn_o_w, L0_ffn_q_norm_w, L0_ffn_k_norm_w, L0_ffn_ffn_norm_w, L0_ffn_gate_w, L0_ffn_wg, L0_ffn_wu, L0_ffn_wd):
    import jax
    import jax.numpy as jnp

    def _L0_xattn_ref(x, weight):
        import jax, jax.numpy as jnp
        import numpy as np
        FP8_MAX = 448.0
        ACT_EPS = 0.0001
        W_EPS = 1e-06
        BLK = 128

        def quant_dequant_act_1x128(x):
            E, M, K = x.shape
            xb = x.reshape(E, M, K // BLK, BLK)
            amax = jnp.max(jnp.abs(xb), axis=-1, keepdims=True)
            safe = jnp.maximum(amax, ACT_EPS)
            q = (xb * (FP8_MAX / safe)).astype(jnp.float8_e4m3fn)
            return (q.astype(jnp.float32) * (safe / FP8_MAX)).reshape(E, M, K)

        def quant_dequant_weight_128x128(w):
            E, N, K = w.shape
            wb = w.reshape(E, N // BLK, BLK, K // BLK, BLK)
            amax = jnp.max(jnp.abs(wb), axis=(2, 4), keepdims=True)
            safe = jnp.maximum(amax, W_EPS)
            q = (wb * (FP8_MAX / safe)).astype(jnp.float8_e4m3fn)
            return (q.astype(jnp.float32) * (safe / FP8_MAX)).reshape(E, N, K)
        xq = quant_dequant_act_1x128(x)
        wq = quant_dequant_weight_128x128(weight)
        return jnp.einsum('emk,enk->emn', xq, wq)

    def _L0_ffn_ref(hidden, attn_norm_w, q_w, k_w, v_w, o_w, q_norm_w, k_norm_w, ffn_norm_w, gate_w, wg, wu, wd):
        import jax, jax.numpy as jnp
        import numpy as np
        ROPE_THETA = 1000000.0
        TOP_K = 2

        def rmsnorm(x, w, eps=1e-06):
            xf = x.astype(jnp.float32)
            n = jax.lax.rsqrt(jnp.mean(xf * xf, axis=-1, keepdims=True) + eps)
            return (xf * n).astype(x.dtype) * w

        def rope_tables(seq_len, head_dim):
            freqs = 1.0 / ROPE_THETA ** (jnp.arange(0, head_dim, 2, dtype=jnp.float32) / head_dim)
            t = jnp.arange(seq_len, dtype=jnp.float32)
            f = jnp.outer(t, freqs)
            return (jnp.cos(f), jnp.sin(f))

        def apply_rope(x, cos, sin):
            half = x.shape[-1] // 2
            x1, x2 = (x[..., :half], x[..., half:])
            c = cos[None, None]
            s = sin[None, None]
            return jnp.concatenate([x1 * c - x2 * s, x2 * c + x1 * s], axis=-1)
        B, S, D = hidden.shape
        hd = q_norm_w.shape[0]
        Hq = q_w.shape[0] // hd
        Hkv = k_w.shape[0] // hd
        n_rep = Hq // Hkv
        h = rmsnorm(hidden, attn_norm_w)
        q = (h @ q_w.T).reshape(B, S, Hq, hd)
        k = (h @ k_w.T).reshape(B, S, Hkv, hd)
        v = (h @ v_w.T).reshape(B, S, Hkv, hd)
        q = rmsnorm(q, q_norm_w).transpose(0, 2, 1, 3)
        k = rmsnorm(k, k_norm_w).transpose(0, 2, 1, 3)
        v = v.transpose(0, 2, 1, 3)
        cos, sin = rope_tables(S, hd)
        q = apply_rope(q, cos, sin)
        k = apply_rope(k, cos, sin)
        k = jnp.repeat(k, n_rep, axis=1)
        v = jnp.repeat(v, n_rep, axis=1)
        scale = 1.0 / jnp.sqrt(jnp.float32(hd))
        scores = jnp.einsum('bhqd,bhkd->bhqk', q, k) * scale
        causal = jnp.tril(jnp.ones((S, S), bool))
        scores = jnp.where(causal[None, None], scores, jnp.finfo(scores.dtype).min)
        attn = jnp.einsum('bhqk,bhkd->bhqd', jax.nn.softmax(scores, axis=-1), v)
        attn = attn.transpose(0, 2, 1, 3).reshape(B, S, Hq * hd)
        hidden = hidden + attn @ o_w.T
        h2 = rmsnorm(hidden, ffn_norm_w)
        T = B * S
        E = gate_w.shape[0]
        tok = h2.reshape(T, D)
        probs = jax.nn.softmax(tok @ gate_w.T, axis=-1)
        topv, topi = jax.lax.top_k(probs, TOP_K)
        topw = topv / (jnp.sum(topv, axis=-1, keepdims=True) + 1e-09)
        combine = jnp.zeros((T, E), tok.dtype).at[jnp.arange(T)[:, None], topi].set(topw)
        eg = jnp.einsum('td,eid->eti', tok, wg)
        eu = jnp.einsum('td,eid->eti', tok, wu)
        eo = jnp.einsum('eti,edi->etd', jax.nn.silu(eg) * eu, wd)
        moe_out = jnp.einsum('te,etd->td', combine, eo).reshape(B, S, D)
        return hidden + moe_out
    x = x + _L0_xattn_ref(_layernorm(x, axis=-1), ctx_2048)
    x = x + _L0_ffn_ref(_layernorm(x, axis=-1), L0_ffn_attn_norm_w, L0_ffn_q_w, L0_ffn_k_w, L0_ffn_v_w, L0_ffn_o_w, L0_ffn_q_norm_w, L0_ffn_k_norm_w, L0_ffn_ffn_norm_w, L0_ffn_gate_w, L0_ffn_wg, L0_ffn_wu, L0_ffn_wd)
    return x

_drawn_inputs = setup_inputs


def setup_inputs(seed=0):
    import zlib

    import numpy as np

    out = dict(_drawn_inputs(seed))
    spreads = {'L0_ffn_attn_norm_w': (1.0, 0.6),
     'L0_ffn_q_norm_w': (1.0, 0.6),
     'L0_ffn_k_norm_w': (1.0, 0.6),
     'L0_ffn_ffn_norm_w': (1.0, 0.6)}
    factors = {'L0_ffn_gate_w': 4.244, 'L0_ffn_wg': 3.793, 'L0_ffn_wu': 3.727, 'L0_ffn_wd': 3.713}
    for name, (base, spread) in spreads.items():
        noise = np.random.default_rng([zlib.crc32(name.encode()), seed]).standard_normal(out[name].shape)
        drawn = base * np.exp(spread * noise) if base else spread * noise
        out[name] = jnp.asarray(drawn.astype(out[name].dtype))
    for name, factor in factors.items():
        out[name] = (out[name] * factor).astype(out[name].dtype)
    return out
```

```python
import concourse.bass as bass
from concourse import mybir
from contextlib import ExitStack

F32 = mybir.dt.float32
F32R = mybir.dt.float32r
BF16 = mybir.dt.bfloat16
U32 = mybir.dt.uint32
I32 = mybir.dt.int32
ALU = mybir.AluOpType
ACT = mybir.ActivationFunctionType
AX = mybir.AxisListType

B, S, D = 4, 512, 512
P = 128
NT = B * S // P
TT = S // P
KC = D // P
HD = 128
HQ, HKV = 16, 4
G = HQ // HKV
E, I = 8, 352
IC = -(-I // P)
IP = IC * P
FP8_MAX = 448.0
RSQRT_MAGIC = float(0x5F3759DF)
EXPONENT_BITS = 0x7F800000
FP8_LEAST_NORMAL = 2.0 ** -6
FP8_ROUND = 1.5 * 2.0 ** 20
SPLITS = ((0, 0), (0, 1), (1, 0))


class Steps:

    def __init__(self, engine, sem, base=0):
        self.engine, self.sem, self.base, self.n = engine, sem, base, 0

    def done(self, ins):
        self.n += 1
        ins.then_inc(self.sem, 1)

    def wait(self):
        self.engine.wait_ge(self.sem, self.base + self.n)

    def chain(self, ins):
        self.done(ins)
        self.wait()


def wait_apart(engine, passed, sem, value):
    engine.wait_ge(sem, value)
    engine.sem_inc(passed, 1)


def rsqrt(nc, chain, out, x, t, u):
    chain(nc.vector.tensor_scalar(u.bitcast(U32), x.bitcast(U32), 1, None, ALU.logical_shift_right))
    chain(nc.vector.tensor_scalar(out.bitcast(I32), u.bitcast(I32), -1.0, RSQRT_MAGIC, ALU.mult, ALU.add))
    for _ in range(3):
        chain(nc.vector.tensor_tensor(t, out, out, ALU.mult))
        chain(nc.vector.scalar_tensor_tensor(u, t, -0.5, x, ALU.mult, ALU.mult))
        chain(nc.vector.scalar_tensor_tensor(out, u, 1.5, out, ALU.add, ALU.mult))


def build(nc, x, ctxT, w_attn, wqkvo, qn, kn, cos, sin, w_ffn, gateT, wexp, ident_d, mask_d, ranklow_d, out):
    ctx = ExitStack()
    with ctx:
        acc = ctx.enter_context(nc.sbuf_tensor("acc", [P, NT, D], F32))
        ident = ctx.enter_context(nc.sbuf_tensor("ident", [P, P], F32))
        identb = ctx.enter_context(nc.sbuf_tensor("identb", [P, P], BF16))
        x1_dram = nc.dram_tensor("x1_scratch", (P, NT, D), F32, kind="Internal").ap()
        hT_dram = nc.dram_tensor("hT_scratch", (B, P, 2 * KC * S), F32, kind="Internal").ap()
        quant_projection(nc, x, ctxT, w_attn, ident_d, acc, ident, identb, x1_dram, hT_dram)
        attention(nc, wqkvo, qn, kn, cos, sin, mask_d, acc, ident, identb, hT_dram)
        with ExitStack() as moe:
            tokT = [moe.enter_context(nc.sbuf_tensor(f"tokT_{n}", [P, KC, B * S], F32R)) for n in ("hi", "lo")]
            combine = moe.enter_context(nc.sbuf_tensor("combine", [P, NT, E], F32))
            router(nc, w_ffn, gateT, ranklow_d, acc, ident, tokT, combine, x1_dram)
            experts(nc, wexp, acc, tokT, combine, out)


def quant_projection(nc, x, ctxT, w_attn, ident_d, acc, ident, identb, x1_dram, hT_dram):
    with ExitStack() as ctx:
        def sb(name, shape, dt=F32):
            return ctx.enter_context(nc.sbuf_tensor(name, shape, dt))

        def sem(name):
            return ctx.enter_context(nc.semaphore(name))

        xs = sb("xs", [P, NT, D])
        cs = sb("cs", [P, B * KC, S])
        wcol = sb("wcol", [P, KC])
        camax = sb("camax", [P, B * KC * 4])
        camaxall = sb("camaxall", [P, B * KC * 4])
        cinv = sb("cinv", [P, B * KC * 4])
        cscale = sb("cscale", [P, B * KC * 4])
        cv = sb("cv", [P, KC * S])
        cm = sb("cm", [P, KC * S])
        cq = sb("cq", [P, KC, S], BF16)
        stats = sb("stats", [P, TT, 6])
        mv = sb("mv", [P, TT, 2])
        var = sb("var", [P, TT])
        rstd = sb("rstd", [P, TT])
        t1 = sb("t1", [P, TT])
        t2 = sb("t2", [P, TT])
        xhat = sb("xhat", [P, TT, D])
        amax = sb("amax", [P, TT * KC])
        ainv = sb("ainv", [P, TT * KC])
        ascale = sb("ascale", [P, TT * KC])
        comb = sb("comb", [P, TT, KC, 4])
        v = sb("v", [P, TT, D])
        m = sb("m", [P, TT, D])
        xq = sb("xq", [P, TT, D], BF16)
        xqT = sb("xqT", [P, TT, KC, P], BF16)
        hn = sb("hn", [P, TT, D])
        hT = [sb(f"hT_{n}", [P, KC, S], F32R) for n in ("hi", "lo")]
        part = [ctx.enter_context(nc.psum_tensor(f"part{i}", [P, S], F32)) for i in range(KC)]
        trq = [ctx.enter_context(nc.psum_tensor(f"trq{i}", [P, KC, P], BF16)) for i in range(2)]
        trh = [ctx.enter_context(nc.psum_tensor(f"trh{i}", [P, S], F32)) for i in range(2)]

        const_in, ctx_in, x_in = sem("const_in"), [sem(f"ctx_in{i}") for i in range(B)], [sem(f"x_in{i}") for i in range(B)]
        identb_ready, ctx_colmax, ctx_max = sem("identb_ready"), sem("ctx_colmax"), sem("ctx_max")
        passed = sem("passed1")
        dve_step, pool_step = sem("dve_step"), sem("pool_step")
        ctx_magic, ctx_quant = sem("ctx_magic"), sem("ctx_quant")
        xhat_ready, v_ready, magic_ready, xq_ready = sem("xhat_ready"), sem("v_ready"), sem("magic_ready"), sem("xq_ready")
        trq_done, xqT_ready, part_done, part_used = sem("trq_done"), sem("xqT_ready"), sem("part_done"), sem("part_used")
        x1_ready, hn_ready, trh_done, hi_ready, lo_ready = (sem(n) for n in ("x1_ready", "hn_ready", "trh_done", "hi_ready", "lo_ready"))
        x1_saved, hT_saved = sem("x1_saved"), sem("hT_saved")
        block = ctx.enter_context(nc.Block())

        @block.sync
        def _(sp):
            for b in range(B):
                sp.dma_start(cs[:, b * KC:(b + 1) * KC, :], ctxT[b].rearrange("(c p) n -> p c n", p=P)).then_inc(ctx_in[b], 16)
            for b in range(B):
                sp.dma_start(xs[:, b * TT:(b + 1) * TT, :],
                             x[b * S:(b + 1) * S, :].rearrange("(t p) d -> p t d", p=P)).then_inc(x_in[b], 16)
            with sp.Fori(0, B) as b:
                sp.wait_ge(x1_ready, b + 1)
                sp.dma_start(x1_dram[:, bass.ds(b * TT, TT), :], xs[:, bass.ds(b * TT, TT), :]).then_inc(x1_saved, 16)
                sp.wait_ge(lo_ready, TT * (b + 1))
                for i in range(2):
                    sp.dma_start(hT_dram[bass.ds(b, 1), :, i * KC * S:(i + 1) * KC * S].rearrange("b p n -> (b p) n"),
                                 hT[i][:, :, :].rearrange("p c n -> p (c n)").bitcast(F32)).then_inc(hT_saved, 16)
            sp.wait_ge(x1_saved, 16 * B)
            sp.wait_ge(hT_saved, 32 * B)

        @block.scalar
        def _(act):
            act.dma_start(wcol[:, :], w_attn).then_inc(const_in, 16)
            act.dma_start(ident[:, :], ident_d).then_inc(const_in, 16)
            act.wait_ge(const_in, 32)
            nc.scalar.activation(identb[:, :], ident[:, :], ACT.Copy).then_inc(identb_ready, 1)
            with act.Fori(0, B) as b:
                act.wait_ge(xhat_ready, b + 1)
                for t in range(TT):
                    for k in range(KC):
                        last = nc.scalar.activation(v[:, t, k * P:(k + 1) * P], xhat[:, t, k * P:(k + 1) * P], ACT.Copy,
                                                    scale=ainv[:, t * KC + k:t * KC + k + 1])
                    last.then_inc(v_ready, 1)
                for t in range(TT):
                    act.wait_ge(trq_done, TT * b + t + 1)
                    nc.scalar.activation(xqT[:, t, :, :], trq[t % 2][:, :, :], ACT.Copy).then_inc(xqT_ready, 1)
                act.wait_ge(hT_saved, 32 * b)
                for t in range(TT):
                    act.wait_ge(trh_done, TT * b + t + 1)
                    for k in range(KC):
                        last = nc.scalar.activation(hT[0][:, k, t * P:(t + 1) * P], trh[t % 2][:, k * P:(k + 1) * P],
                                                    ACT.Copy, scale=wcol[:, k:k + 1])
                    last.then_inc(hi_ready, 1)

        @block.gpsimd
        def _(pool):
            pool.wait_ge(ctx_colmax, 1)
            nc.gpsimd.partition_all_reduce(camaxall[:, :], camax[:, :], P, bass.bass_isa.ReduceOp.max).then_inc(ctx_max, 1)
            with pool.Fori(0, B) as b:
                pool.wait_ge(ctx_magic, b + 1)
                nc.gpsimd.tensor_tensor(cv[:, :], cv[:, :], cm[:, :], ALU.add).then_inc(pool_step, 1)
                pool.wait_ge(pool_step, (TT + 1) * b + 1)
                nc.gpsimd.tensor_tensor(cq[:, :, :].rearrange("p c n -> p (c n)"), cv[:, :], cm[:, :], ALU.subtract).then_inc(ctx_quant, 1)
                for t in range(TT):
                    pool.wait_ge(magic_ready, TT * b + t + 1)
                    nc.gpsimd.tensor_tensor(v[:, t, :], v[:, t, :], m[:, t, :], ALU.add).then_inc(pool_step, 1)
                    pool.wait_ge(pool_step, (TT + 1) * b + t + 2)
                    nc.gpsimd.tensor_tensor(xq[:, t, :], v[:, t, :], m[:, t, :], ALU.subtract).then_inc(xq_ready, 1)

        @block.tensor
        def _(pe):
            pe.wait_ge(identb_ready, 1)
            with pe.Fori(0, B) as b:
                for t in range(TT):
                    pe.wait_ge(xq_ready, TT * b + t + 1)
                    if t >= 2:
                        pe.wait_ge(xqT_ready, TT * b + t - 1)
                    for k in range(KC):
                        last = nc.tensor.transpose(trq[t % 2][:, k, :], xq[:, t, k * P:(k + 1) * P], identb[:, :])
                    last.then_inc(trq_done, 1)
                pe.wait_ge(ctx_quant, b + 1)
                for t in range(TT):
                    pe.wait_ge(xqT_ready, TT * b + t + 1)
                    for k in range(KC):
                        if t:
                            pe.wait_ge(part_used, TT * KC * b + KC * (t - 1) + k + 1)
                        nc.tensor.matmul(part[k][:, :], xqT[:, t, k, :], cq[:, k, :], start=True, stop=True).then_inc(part_done, 1)
                for t in range(TT):
                    pe.wait_ge(hn_ready, TT * b + t + 1)
                    if t >= 2:
                        pe.wait_ge(lo_ready, TT * b + t - 1)
                    for k in range(KC):
                        last = nc.tensor.transpose(trh[t % 2][:, k * P:(k + 1) * P], hn[:, t, k * P:(k + 1) * P], ident[:, :])
                    last.then_inc(trh_done, 1)

        @block.vector
        def _(dve):
            pre = Steps(dve, dve_step)
            for b in range(B):
                dve.wait_ge(ctx_in[b], 16)
                last = nc.vector.tensor_reduce(camax[:, b * 16:(b + 1) * 16],
                                               cs[:, b * KC:(b + 1) * KC, :].rearrange("p c (n k) -> p (c n) k", k=P),
                                               AX.X, ALU.max, apply_absolute_value=True)
            last.then_inc(ctx_colmax, 1)
            dve.wait_ge(ctx_max, 1)
            pre.chain(nc.vector.tensor_scalar(camax[:, :], camaxall[:, :], 1e-6, None, ALU.max))
            pre.chain(nc.vector.reciprocal(cinv[:, :], camax[:, :]))
            pre.chain(nc.vector.tensor_scalar(cinv[:, :], cinv[:, :], FP8_MAX, None, ALU.mult))
            pre.chain(nc.vector.tensor_scalar(cscale[:, :], camax[:, :], 1.0 / FP8_MAX, None, ALU.mult))
            for b in range(B):
                dve.wait_ge(x_in[b], 16)
            dve.wait_ge(const_in, 32)
            per_batch = LOOP1_STEPS
            with dve.Fori(0, B) as b:
                own = Steps(dve, dve_step, pre.n + b * per_batch)

                def moments(tile):
                    for t in range(TT):
                        own.done(nc.vector.bn_stats(stats[:, t, :], tile(t)))
                    wait_apart(dve, passed, dve_step, own.base + own.n)
                    for t in range(TT):
                        own.done(nc.vector.bn_aggr(mv[:, t, :], stats[:, t, :]))
                    own.wait()

                moments(lambda t: xs[:, bass.ds(b * TT + t, 1), :].rearrange("p a d -> p (a d)"))
                own.chain(nc.vector.tensor_scalar(var[:, :], mv[:, :, 1], 1e-5, None, ALU.add))
                rsqrt(nc, own.chain, rstd[:, :], var[:, :], t1[:, :], t2[:, :])
                for t in range(TT):
                    own.chain(nc.vector.tensor_scalar(xhat[:, t, :], xs[:, bass.ds(b * TT + t, 1), :].rearrange("p a d -> p (a d)"),
                                                      mv[:, t, 0:1], rstd[:, t:t + 1], ALU.subtract, ALU.mult))
                own.chain(nc.vector.tensor_reduce(amax[:, :], xhat[:, :, :].rearrange("p t (k d) -> p (t k) d", d=P), AX.X, ALU.max,
                                                  apply_absolute_value=True))
                own.chain(nc.vector.tensor_scalar(amax[:, :], amax[:, :], 1e-4, None, ALU.max))
                own.chain(nc.vector.reciprocal(ainv[:, :], amax[:, :]))
                nc.vector.tensor_scalar(ainv[:, :], ainv[:, :], FP8_MAX, None, ALU.mult).then_inc(xhat_ready, 1)
                cblock = cs[:, bass.ds(b * KC, KC), :].rearrange("p c (n k) -> p (c n) k", k=P)
                own.chain(nc.vector.tensor_tensor(cv[:, :].rearrange("p (a k) -> p a k", k=P), cblock,
                                                  cinv[:, bass.ds(b * 16, 16)].unsqueeze(2).broadcast_to([P, 16, P]), ALU.mult))
                own.chain(nc.vector.tensor_scalar(cm[:, :].bitcast(U32), cv[:, :].bitcast(U32), EXPONENT_BITS, None, ALU.bitwise_and))
                nc.vector.tensor_scalar(cm[:, :], cm[:, :], FP8_LEAST_NORMAL, FP8_ROUND, ALU.max, ALU.mult).then_inc(ctx_magic, 1)
                own.chain(nc.vector.tensor_scalar(ascale[:, :], amax[:, :], 1.0 / FP8_MAX, None, ALU.mult))
                for t in range(TT):
                    own.done(nc.vector.tensor_tensor(comb[:, t, :, :], cscale[:, bass.ds(b * 16, 16)].rearrange("p (k n) -> p k n", n=4),
                                                     ascale[:, t * KC:(t + 1) * KC].unsqueeze(2).broadcast_to([P, KC, 4]), ALU.mult))
                for t in range(TT):
                    dve.wait_ge(v_ready, TT * b + t + 1)
                    own.chain(nc.vector.tensor_scalar(m[:, t, :].bitcast(U32), v[:, t, :].bitcast(U32), EXPONENT_BITS, None, ALU.bitwise_and))
                    nc.vector.tensor_scalar(m[:, t, :], m[:, t, :], FP8_LEAST_NORMAL, FP8_ROUND, ALU.max, ALU.mult).then_inc(magic_ready, 1)
                for t in range(TT):
                    for k in range(KC):
                        dve.wait_ge(part_done, TT * KC * b + KC * t + k + 1)
                        if k:
                            dve.wait_ge(part_used, TT * KC * b + KC * t + k)
                        for n in range(4):
                            x1 = xs[:, bass.ds(b * TT + t, 1), n * P:(n + 1) * P].rearrange("p a d -> p (a d)")
                            last = nc.vector.scalar_tensor_tensor(x1, part[k][:, n * P:(n + 1) * P], comb[:, t, k, n:n + 1], x1,
                                                                  ALU.mult, ALU.add)
                        last.then_inc(part_used, 1)
                wait_apart(dve, passed, part_used, TT * KC * (b + 1))
                moments(lambda t: xs[:, bass.ds(b * TT + t, 1), :].rearrange("p a d -> p (a d)"))
                own.chain(nc.vector.tensor_scalar(var[:, :], mv[:, :, 1], 1e-5, None, ALU.add))
                rsqrt(nc, own.chain, rstd[:, :], var[:, :], t1[:, :], t2[:, :])
                for t in range(TT):
                    own.done(nc.vector.tensor_scalar(acc[:, bass.ds(b * TT + t, 1), :].rearrange("p a d -> p (a d)"),
                                                     xs[:, bass.ds(b * TT + t, 1), :].rearrange("p a d -> p (a d)"),
                                                     mv[:, t, 0:1], rstd[:, t:t + 1], ALU.subtract, ALU.mult))
                own.chain(nc.vector.tensor_tensor(t1[:, :], rstd[:, :], rstd[:, :], ALU.mult))
                own.chain(nc.vector.tensor_tensor(var[:, :], t1[:, :], mv[:, :, 1], ALU.mult))
                nc.vector.tensor_scalar(var[:, :], var[:, :], 1e-6, None, ALU.add).then_inc(x1_ready, 1)
                dve.wait_ge(x1_ready, b + 1)
                rsqrt(nc, own.chain, rstd[:, :], var[:, :], t1[:, :], t2[:, :])
                for t in range(TT):
                    nc.vector.tensor_scalar(hn[:, t, :], acc[:, bass.ds(b * TT + t, 1), :].rearrange("p a d -> p (a d)"),
                                            rstd[:, t:t + 1], None, ALU.mult).then_inc(hn_ready, 1)
                for t in range(TT):
                    dve.wait_ge(hi_ready, TT * b + t + 1)
                    for k in range(KC):
                        last = nc.vector.scalar_tensor_tensor(hT[1][:, k, t * P:(t + 1) * P], trh[t % 2][:, k * P:(k + 1) * P],
                                                              wcol[:, k:k + 1], hT[0][:, k, t * P:(t + 1) * P].bitcast(F32),
                                                              ALU.mult, ALU.subtract)
                    last.then_inc(lo_ready, 1)
                assert own.n == per_batch, own.n


LOOP1_STEPS = 75
ATTN_STEPS = 120


def attention(nc, wqkvo, qn, kn, cos, sin, mask_d, acc, ident, identb, hT_dram):
    with ExitStack() as ctx:
        def sb(name, shape, dt=F32):
            return ctx.enter_context(nc.sbuf_tensor(name, shape, dt))

        def sem(name):
            return ctx.enter_context(nc.semaphore(name))

        CH = 512
        NCH, RING, QKV = 10, 5, 6
        R = G * HD + HD
        KEYS = [(q + 1) * P for q in range(TT)]
        P_AT = [sum(KEYS[:q]) for q in range(TT)]
        QS = [S - j * P for j in range(TT)]
        PT_AT = [sum(QS[:j]) for j in range(TT)]

        hT = [sb(f"hTb{i}", [P, 2, KC, S], F32R) for i in range(2)]
        stage = [sb(f"stage{i}", [P, CH]) for i in range(RING)]
        w = [sb(f"w_{n}", [P, NCH * CH], F32R) for n in ("hi", "lo")]
        tab = {(n, f): sb(f"tab_{n}_{f}", [P, TT, HD]) for n in "qk" for f in "cs"}
        sq = sb("sq", [P, R])
        rot = [sb(f"rot{i}", [P, R]) for i in range(2)]
        r = sb("r", [P, TT, R])
        qT = [sb(f"qT_{n}", [P, G, S], F32R) for n in ("hi", "lo")]
        kT = [sb(f"kT_{n}", [P, S], F32R) for n in ("hi", "lo")]
        v = [[sb(f"v{i}_{n}", [P, TT, HD], F32R) for n in ("hi", "lo")] for i in range(2)]
        prob = [sb(f"prob{i}", [P, sum(KEYS)]) for i in range(2)]
        pT = [sb(f"pT_{n}", [P, sum(QS)], F32R) for n in ("hi", "lo")]
        aT = [sb(f"aT_{n}", [P, G, S], F32R) for n in ("hi", "lo")]
        mask = sb("mask", [P, P], BF16)
        ssum = sb("ssum", [P, TT, G + 1])
        rn = sb("rn", [P, TT, G + 1])
        n1, n2 = sb("n1", [P, TT * (G + 1)]), sb("n2", [P, TT * (G + 1)])
        scale = [sb(f"scale{i}", [P, TT, G]) for i in range(2)]
        nscale = [sb(f"nscale{i}", [P, TT, G]) for i in range(2)]
        top, bias = sb("top", [P, G * TT]), sb("bias", [P, G * TT])
        total, rtotal = sb("total", [P, G * TT]), sb("rtotal", [P, G * TT])
        bank = [ctx.enter_context(nc.psum_tensor(f"bank{i}", [P, S], F32)) for i in range(8)]
        TR, SC, PT, PV = 2, 3, 5, 7

        const_in, passed, maskf_ready = sem("const_in2"), sem("passed2"), sem("maskf_ready")
        ht_in = [sem(f"ht_in{i}") for i in range(2)]
        stage_in = [sem(f"stage_in{i}") for i in range(RING)]
        w_hi, w_split = sem("w_hi"), sem("w_split")
        projq, projkv = sem("projq"), sem("projkv")
        q_squared, kv_squared, ssum_ready = sem("q_squared"), sem("kv_squared"), sem("ssum_ready")
        q_rotated, kv_rotated, rope_added, k_ready = sem("q_rotated"), sem("kv_rotated"), sem("rope_added"), sem("k_ready")
        qk_tr, qk_hi, qk_lo = sem("qk_tr"), sem("qk_hi"), sem("qk_lo")
        scored, biased, exp_done, inverted, prob_ready = sem("scored"), sem("biased"), sem("exp_done"), sem("inverted"), sem("prob_ready")
        pt_tr, pt_hi, pt_lo, pv_step = sem("pt_tr"), sem("pt_hi"), sem("pt_lo"), sem("pv_step")
        at_hi, at_lo, o_done, o_added = sem("at_hi"), sem("at_lo"), sem("o_done"), sem("o_added")
        dve_own = sem("dve_own")
        FREE = {exp_done: 2, pt_lo: 2, pv_step: 4, at_lo: 1, o_added: 1, o_done: 1, projkv: 1, q_rotated: 1, q_squared: 1,
                kv_rotated: 1, kv_squared: 1, ssum_ready: 1, rope_added: 2, qk_lo: 1}
        block = ctx.enter_context(nc.Block())

        def wq(i, k):
            return w[i][:, k * CH:(k + 1) * CH]

        def wkv(i, k):
            return w[i][:, G * CH + k * 2 * HD:G * CH + (k + 1) * 2 * HD]

        def wo(i, h):
            return w[i][:, (QKV + h) * CH:(QKV + h + 1) * CH]

        @block.sync
        def _(sp):
            def load(g, c, slot):
                sp.dma_start(stage[slot][:, :], wqkvo[bass.ds(g, 1), c, :, :].rearrange("g p n -> (g p) n")).then_inc(stage_in[slot], 16)

            for i, (norm, table) in enumerate(((qn, cos), (kn, sin))):
                sp.dma_start(prob[i][:, 0:HD], norm.rearrange("(a d) -> a d", a=1).broadcast_to([P, HD])).then_inc(const_in, 16)
                sp.dma_start(prob[i][:, 256:256 + TT * HD // 2], table).then_inc(const_in, 16)
            sp.dma_start(prob[0][:, 1024:1024 + P], mask_d).then_inc(const_in, 16)
            for s in range(QKV):
                if s >= RING:
                    sp.wait_ge(w_split, s - RING + 1)
                load(0, s, s % RING)
            with sp.Fori(0, HKV) as g:
                for i in range(NCH):
                    c = (QKV + i) % NCH
                    sp.wait_ge(w_split, NCH * g + QKV + i - RING + 1)
                    load(g if i < NCH - QKV else g + 1, c, (QKV + i) % RING)
            sp.wait_ge(w_split, NCH * HKV + QKV)

        @block.gpsimd
        def _(pool):
            def split(seq, c, slot, nth):
                wait_apart(pool, passed, stage_in[slot], 16 * nth)
                nc.gpsimd.tensor_copy(w[0][:, c * CH:(c + 1) * CH], stage[slot][:, :]).then_inc(w_hi, 1)
                pool.wait_ge(w_hi, seq + 1)
                nc.gpsimd.tensor_tensor(w[1][:, c * CH:(c + 1) * CH], stage[slot][:, :], w[0][:, c * CH:(c + 1) * CH].bitcast(F32),
                                        ALU.subtract).then_inc(w_split, 1)

            def add_rope(j, t):
                pool.wait_ge(kv_rotated, FREE[kv_rotated] + TT * j + t + 1)
                nc.gpsimd.tensor_tensor(r[:, t, :], r[:, t, :], rot[t % 2][:, :], ALU.add).then_inc(rope_added, 1)

            def normalise(it, h, q):
                wait_apart(pool, passed, inverted, 16 * it + 4 * h + q + 1)
                p = prob[h % 2][:, P_AT[q]:P_AT[q] + KEYS[q]]
                nc.gpsimd.tensor_scalar(p, p, rtotal[:, 4 * h + q:4 * h + q + 1], None, ALU.mult).then_inc(prob_ready, 1)

            pool.sem_inc(rope_added, FREE[rope_added])
            for s in range(QKV):
                split(s, s, s % RING, s // RING + 1)
            with pool.Fori(0, HKV) as g:
                for t in range(TT):
                    add_rope(4 * g, t)
                pool.wait_ge(o_done, FREE[o_done] + 4 * TT * g)
                for i in range(NCH - QKV):
                    s = QKV + i
                    split(NCH * g + s, s, s % RING, 2 * g + s // RING + 1)
                for b in range(B):
                    it = 4 * g + b
                    if b == B - 1:
                        pool.wait_ge(projkv, FREE[projkv] + 4 * TT * (g + 1))
                    for h in range(G):
                        for q in range(3):
                            normalise(it, h, q)
                        if b < B - 1:
                            add_rope(it + 1, h)
                        normalise(it, h, 3)
                        if b == B - 1:
                            for c in (2 * h, 2 * h + 1):
                                if c < QKV:
                                    s = NCH + c
                                    split(NCH * g + s, c, s % RING, 2 * g + s // RING + 1)

        @block.tensor
        def _(pe):
            def project(g, b, t, kv):
                j = 4 * g + b
                if t == 0 and not kv:
                    pe.wait_ge(ht_in[b % 2], 16 * (2 * g + b // 2 + 1))
                if b == 0 and t == 0:
                    pe.wait_ge(w_split, NCH * g + (QKV if kv else G))
                if kv:
                    pe.wait_ge(kv_rotated, FREE[kv_rotated] + TT * j + t)
                else:
                    pe.wait_ge(q_rotated, FREE[q_rotated] + TT * j + t)
                if t == 0:
                    pe.wait_ge(o_added, FREE[o_added] + (TT * j if b == 0 else TT * (j - 1)))
                o = bank[1][:, 0:2 * HD] if kv else bank[0][:, :]
                for k in range(KC):
                    for n, (a, c) in enumerate(SPLITS):
                        last = nc.tensor.matmul(o, hT[b % 2][:, a, k, t * P:(t + 1) * P], wkv(c, k) if kv else wq(c, k),
                                                start=(k == 0 and n == 0), stop=(k == KC - 1 and n == 2))
                last.then_inc(projkv if kv else projq, 1)

            def transpose_qk(j, i):
                if i == 0:
                    pe.wait_ge(k_ready, j + 1)
                pe.wait_ge(qk_lo, FREE[qk_lo] + (G + 1) * j + i)
                at = G * HD if i == 0 else (i - 1) * HD
                for t in range(TT):
                    last = nc.tensor.transpose(bank[TR][:, t * P:(t + 1) * P], r[:, t, at:at + HD], ident[:, :])
                last.then_inc(qk_tr, 1)

            def score(it, h, q):
                if q == 0:
                    pe.wait_ge(qk_lo, FREE[qk_lo] + (G + 1) * it + h + 2)
                pe.wait_ge(exp_done, FREE[exp_done] + 16 * it + 4 * h + q - 1)
                o = bank[SC + q % 2]
                for n, (a, c) in enumerate(SPLITS):
                    nc.tensor.matmul(o[:, 0:KEYS[q]], qT[a][:, h, q * P:(q + 1) * P], kT[c][:, 0:KEYS[q]], start=(n == 0), stop=False)
                nc.tensor.matmul(o[:, q * P:(q + 1) * P], identb[:, :], mask[:, :], start=False, stop=True).then_inc(scored, 1)

            def transpose_p(it, h, j):
                if j == 0:
                    pe.wait_ge(prob_ready, 16 * it + 4 * h + TT)
                pe.wait_ge(pt_lo, FREE[pt_lo] + 16 * it + 4 * h + j - 1)
                for q in range(j, TT):
                    last = nc.tensor.transpose(bank[PT + j % 2][:, (q - j) * P:(q - j + 1) * P],
                                               prob[h % 2][:, P_AT[q] + j * P:P_AT[q] + (j + 1) * P], ident[:, :])
                last.then_inc(pt_tr, 1)

            def values(it, b, h, j):
                if h == 0 and j == 0:
                    pe.wait_ge(kv_rotated, FREE[kv_rotated] + TT * (it + 1))
                if j == 0:
                    pe.wait_ge(at_lo, FREE[at_lo] + G * it + h)
                pe.wait_ge(pt_lo, FREE[pt_lo] + 16 * it + 4 * h + j + 1)
                for n, (a, c) in enumerate(SPLITS):
                    last = nc.tensor.matmul(bank[PV][:, j * P:S], v[b % 2][a][:, j, :], pT[c][:, PT_AT[j]:PT_AT[j] + QS[j]],
                                            start=(j == 0 and n == 0), stop=(j == TT - 1 and n == 2))
                last.then_inc(pv_step, 1)

            def output(g, b, t):
                it = 4 * g + b
                if t == 0:
                    pe.wait_ge(w_split, NCH * (g + 1))
                    pe.wait_ge(at_lo, FREE[at_lo] + G * (it + 1))
                if t < 2 and b < B - 1:
                    if t == 0:
                        pe.wait_ge(q_rotated, FREE[q_rotated] + TT * (it + 2))
                    else:
                        pe.wait_ge(kv_rotated, FREE[kv_rotated] + TT * (it + 2))
                pe.wait_ge(o_added, FREE[o_added] + TT * it + max(t - 1, 0))
                for h in range(G):
                    for n, (a, c) in enumerate(SPLITS):
                        last = nc.tensor.matmul(bank[t % 2][:, :], aT[a][:, h, t * P:(t + 1) * P], wo(c, h),
                                                start=(h == 0 and n == 0), stop=(h == G - 1 and n == 2))
                last.then_inc(o_done, 1)

            pe.sem_inc(projkv, FREE[projkv])
            pe.sem_inc(o_done, FREE[o_done])
            pe.sem_inc(pv_step, FREE[pv_step])
            pe.wait_ge(maskf_ready, 1)
            with pe.Fori(0, HKV) as g:
                for t in range(TT):
                    project(g, 0, t, False)
                    project(g, 0, t, True)
                for i in range(G + 1):
                    transpose_qk(4 * g, i)
                for b in range(B):
                    it, more = 4 * g + b, b < B - 1
                    for h in range(G):
                        score(it, h, 0)
                        score(it, h, 1)
                        if h:
                            transpose_p(it, h - 1, 0)
                            transpose_p(it, h - 1, 1)
                        if more:
                            project(g, b + 1, h, False)
                        score(it, h, 2)
                        if h:
                            values(it, b, h - 1, 0)
                            transpose_p(it, h - 1, 2)
                            values(it, b, h - 1, 1)
                            transpose_p(it, h - 1, 3)
                        score(it, h, 3)
                        if more:
                            project(g, b + 1, h, True)
                        if h:
                            values(it, b, h - 1, 2)
                            values(it, b, h - 1, 3)
                    h = G - 1
                    transpose_p(it, h, 0)
                    transpose_p(it, h, 1)
                    if more:
                        transpose_qk(it + 1, 0)
                    values(it, b, h, 0)
                    transpose_p(it, h, 2)
                    values(it, b, h, 1)
                    transpose_p(it, h, 3)
                    if more:
                        transpose_qk(it + 1, 1)
                    values(it, b, h, 2)
                    values(it, b, h, 3)
                    for t in range(TT):
                        if more and t < G - 1:
                            transpose_qk(it + 1, 2 + t)
                        output(g, b, t)

        @block.scalar
        def _(act):
            def load_hT(bn, slot):
                act.dma_start(hT[slot][:, :, :, :].rearrange("p a k n -> p (a k n)").bitcast(F32), hT_dram[bn]).then_inc(ht_in[slot], 16)

            def square_q(j, t):
                act.wait_ge(projq, TT * j + t + 1)
                act.wait_ge(ssum_ready, FREE[ssum_ready] + TT * j + t)
                nc.scalar.activation(sq[:, 0:G * HD], bank[0][:, :], ACT.Square).then_inc(q_squared, 1)

            def square_kv(j, b, t):
                act.wait_ge(projkv, FREE[projkv] + TT * j + t + 1)
                nc.scalar.activation(v[b % 2][0][:, t, :], bank[1][:, HD:2 * HD], ACT.Copy)
                nc.scalar.activation(sq[:, G * HD:R], bank[1][:, 0:HD], ACT.Square).then_inc(kv_squared, 1)
                if t == TT - 1:
                    load_hT((b + 2) % B, b % 2)

            def exponentials(it, b, h, q):
                act.wait_ge(biased, 16 * it + 4 * h + q + 1)
                nc.scalar.activation(prob[h % 2][:, P_AT[q]:P_AT[q] + KEYS[q]], bank[SC + q % 2][:, 0:KEYS[q]], ACT.Exp,
                                     bias=bias[:, 4 * h + q:4 * h + q + 1], scale=scale[b % 2][:, q, h:h + 1],
                                     accum_out=total[:, 4 * h + q:4 * h + q + 1]).then_inc(exp_done, 1)

            def hi_p(it, h, j):
                act.wait_ge(pt_tr, 16 * it + 4 * h + j + 1)
                act.wait_ge(pv_step, FREE[pv_step] + 16 * it + 4 * h + j - 3)
                nc.scalar.activation(pT[0][:, PT_AT[j]:PT_AT[j] + QS[j]], bank[PT + j % 2][:, 0:QS[j]], ACT.Copy).then_inc(pt_hi, 1)

            def hi_attn(it, h):
                act.wait_ge(pv_step, FREE[pv_step] + 16 * it + 4 * h + 4)
                if h == 0:
                    act.wait_ge(o_done, FREE[o_done] + TT * it)
                nc.scalar.activation(aT[0][:, h, :], bank[PV][:, :], ACT.Copy).then_inc(at_hi, 1)

            def hi_qk(j, i):
                act.wait_ge(qk_tr, (G + 1) * j + i + 1)
                o = kT[0][:, :] if i == 0 else qT[0][:, i - 1, :]
                nc.scalar.activation(o, bank[TR][:, :], ACT.Copy).then_inc(qk_hi, 1)

            for s in (exp_done, q_squared, kv_squared):
                act.sem_inc(s, FREE[s])
            load_hT(0, 0)
            load_hT(1, 1)
            with act.Fori(0, HKV) as g:
                for t in range(TT):
                    square_q(4 * g, t)
                    square_kv(4 * g, 0, t)
                for i in range(G + 1):
                    hi_qk(4 * g, i)
                for b in range(B):
                    it, more = 4 * g + b, b < B - 1
                    for h in range(G):
                        exponentials(it, b, h, 0)
                        exponentials(it, b, h, 1)
                        if h:
                            hi_p(it, h - 1, 0)
                            hi_p(it, h - 1, 1)
                        if more:
                            square_q(it + 1, h)
                        exponentials(it, b, h, 2)
                        if h:
                            hi_p(it, h - 1, 2)
                            hi_p(it, h - 1, 3)
                        exponentials(it, b, h, 3)
                        if more:
                            square_kv(it + 1, b + 1, h)
                        if h:
                            hi_attn(it, h - 1)
                    h = G - 1
                    hi_p(it, h, 0)
                    hi_p(it, h, 1)
                    if more:
                        hi_qk(it + 1, 0)
                    hi_p(it, h, 2)
                    hi_p(it, h, 3)
                    if more:
                        hi_qk(it + 1, 1)
                    hi_attn(it, h)
                    if more:
                        for i in range(2, G + 1):
                            hi_qk(it + 1, i)
            for slot in range(2):
                act.wait_ge(ht_in[slot], 16 * (2 * HKV + 1))

        @block.vector
        def _(dve):
            def rotate(j, t, kv):
                n, at, heads, name = (bank[1][:, 0:HD], G * HD, 1, "k") if kv else (bank[0][:, :], 0, G, "q")
                src = n.rearrange("p (h d) -> p h d", h=heads)
                if kv:
                    dve.wait_ge(kv_squared, FREE[kv_squared] + TT * j + t + 1)
                else:
                    dve.wait_ge(q_squared, FREE[q_squared] + TT * j + t + 1)
                    dve.wait_ge(rope_added, FREE[rope_added] + TT * j + t - 1)
                o = r[:, t, at:at + heads * HD].rearrange("p (h d) -> p h d", h=heads)
                o2 = rot[t % 2][:, at:at + heads * HD].rearrange("p (h d) -> p h d", h=heads)
                H = HD // 2
                c, s = tab[name, "c"][:, t, :], tab[name, "s"][:, t, :]
                nc.vector.tensor_tensor(o, src, c.unsqueeze(1).broadcast_to([P, heads, HD]), ALU.mult)
                nc.vector.tensor_tensor(o2[:, :, 0:H], src[:, :, H:HD], s[:, 0:H].unsqueeze(1).broadcast_to([P, heads, H]), ALU.mult)
                last = nc.vector.tensor_tensor(o2[:, :, H:HD], src[:, :, 0:H], s[:, H:HD].unsqueeze(1).broadcast_to([P, heads, H]), ALU.mult)
                if not kv:
                    last.then_inc(q_rotated, 1)

            def rest_kv(j, b, t):
                rotate(j, t, True)
                nc.vector.tensor_tensor(v[b % 2][1][:, t, :], bank[1][:, HD:2 * HD], v[b % 2][0][:, t, :].bitcast(F32),
                                        ALU.subtract).then_inc(kv_rotated, 1)
                nc.vector.tensor_reduce(ssum[:, t, :], sq[:, :].rearrange("p (h d) -> p h d", d=HD), AX.X, ALU.add).then_inc(ssum_ready, 1)

            def finish_norms(j, b, own):
                dve.wait_ge(ssum_ready, FREE[ssum_ready] + TT * (j + 1))
                flat = ssum[:, :, :].rearrange("p t h -> p (t h)")
                own.chain(nc.vector.tensor_scalar(flat, flat, 1.0 / HD, 1e-6, ALU.mult, ALU.add))
                rsqrt(nc, own.chain, rn[:, :, :].rearrange("p t h -> p (t h)"), flat, n1[:, :], n2[:, :])
                own.done(nc.vector.tensor_scalar(scale[b % 2][:, :, :], rn[:, :, 0:G], HD ** -0.5, None, ALU.mult))
                own.done(nc.vector.tensor_scalar(nscale[b % 2][:, :, :], rn[:, :, 0:G], -HD ** -0.5, None, ALU.mult))
                dve.wait_ge(rope_added, FREE[rope_added] + TT * (j + 1))
                k = r[:, :, G * HD:R]
                nc.vector.tensor_tensor(k, k, rn[:, :, G:G + 1].broadcast_to([P, TT, HD]), ALU.mult).then_inc(k_ready, 1)

            def maxima(it, b, h, q, own):
                n = 4 * h + q
                dve.wait_ge(scored, 16 * it + n + 1)
                if n == 0:
                    own.wait()
                own.chain(nc.vector.tensor_reduce(top[:, n:n + 1], bank[SC + q % 2][:, 0:KEYS[q]], AX.X, ALU.max))
                nc.vector.tensor_tensor(bias[:, n:n + 1], top[:, n:n + 1], nscale[b % 2][:, q, h:h + 1], ALU.mult).then_inc(biased, 1)

            def invert(it, h, q):
                n = 4 * h + q
                dve.wait_ge(exp_done, FREE[exp_done] + 16 * it + n + 1)
                nc.vector.reciprocal(rtotal[:, n:n + 1], total[:, n:n + 1]).then_inc(inverted, 1)

            def lo_p(it, h, j):
                dve.wait_ge(pt_hi, 16 * it + 4 * h + j + 1)
                sl = slice(PT_AT[j], PT_AT[j] + QS[j])
                nc.vector.tensor_tensor(pT[1][:, sl], bank[PT + j % 2][:, 0:QS[j]], pT[0][:, sl].bitcast(F32), ALU.subtract).then_inc(pt_lo, 1)

            def lo_attn(it, h):
                dve.wait_ge(at_hi, G * it + h + 1)
                nc.vector.tensor_tensor(aT[1][:, h, :], bank[PV][:, :], aT[0][:, h, :].bitcast(F32), ALU.subtract).then_inc(at_lo, 1)

            def lo_qk(j, i):
                dve.wait_ge(qk_hi, (G + 1) * j + i + 1)
                hi, lo = (kT[0][:, :], kT[1][:, :]) if i == 0 else (qT[0][:, i - 1, :], qT[1][:, i - 1, :])
                nc.vector.tensor_tensor(lo, bank[TR][:, :], hi.bitcast(F32), ALU.subtract).then_inc(qk_lo, 1)

            def add_output(it, b, t):
                dve.wait_ge(o_done, FREE[o_done] + TT * it + t + 1)
                a = acc[:, b * TT + t, :]
                nc.vector.tensor_tensor(a, bank[t % 2][:, :], a, ALU.add).then_inc(o_added, 1)

            for s in (pt_lo, at_lo, o_added, q_rotated, kv_rotated, ssum_ready, qk_lo):
                dve.sem_inc(s, FREE[s])
            pre = Steps(dve, dve_own)
            if True:
                H = HD // 2
                wrow = {n: prob[i][:, 0:HD] for i, n in enumerate("qk")}
                cs_t, sn_t = prob[0][:, 256:256 + TT * H], prob[1][:, 256:256 + TT * H]
                maskf = prob[0][:, 1024:1024 + P]
                dve.wait_ge(const_in, 16 * 5)
                nc.vector.tensor_copy(mask[:, :], maskf).then_inc(maskf_ready, 1)
                for n in "qk":
                    for t in range(TT):
                        c, s = cs_t[:, t * H:(t + 1) * H], sn_t[:, t * H:(t + 1) * H]
                        for a in range(2):
                            own_w, other_w = wrow[n][:, a * H:(a + 1) * H], wrow[n][:, (1 - a) * H:(2 - a) * H]
                            pre.done(nc.vector.tensor_tensor(tab[n, "c"][:, t, a * H:(a + 1) * H], c, own_w, ALU.mult))
                            pre.done(nc.vector.scalar_tensor_tensor(tab[n, "s"][:, t, a * H:(a + 1) * H], s, 1.0 if a else -1.0, other_w,
                                                                    ALU.mult, ALU.mult))
                pre.wait()
            with dve.Fori(0, HKV) as g:
                own = Steps(dve, dve_own, pre.n + g * ATTN_STEPS)
                for t in range(TT):
                    rotate(4 * g, t, False)
                    rest_kv(4 * g, 0, t)
                finish_norms(4 * g, 0, own)
                for i in range(G + 1):
                    lo_qk(4 * g, i)
                for b in range(B):
                    it, more = 4 * g + b, b < B - 1
                    for h in range(G):
                        maxima(it, b, h, 0, own)
                        maxima(it, b, h, 1, own)
                        if h:
                            lo_p(it, h - 1, 0)
                            lo_p(it, h - 1, 1)
                        invert(it, h, 0)
                        invert(it, h, 1)
                        if more:
                            rotate(it + 1, h, False)
                        maxima(it, b, h, 2, own)
                        if h:
                            lo_p(it, h - 1, 2)
                            lo_p(it, h - 1, 3)
                        invert(it, h, 2)
                        maxima(it, b, h, 3, own)
                        if more:
                            rest_kv(it + 1, b + 1, h)
                        invert(it, h, 3)
                        if h:
                            lo_attn(it, h - 1)
                    h = G - 1
                    if more:
                        finish_norms(it + 1, b + 1, own)
                    lo_p(it, h, 0)
                    lo_p(it, h, 1)
                    if more:
                        lo_qk(it + 1, 0)
                    lo_p(it, h, 2)
                    lo_p(it, h, 3)
                    if more:
                        lo_qk(it + 1, 1)
                    lo_attn(it, h)
                    for t in range(TT):
                        if more and t < G - 1:
                            lo_qk(it + 1, 2 + t)
                        add_output(it, b, t)
                assert own.n == ATTN_STEPS, own.n



def router(nc, w_ffn, gateT, ranklow_d, acc, ident, tokT, combine, x1_dram):
    with ExitStack() as ctx:
        def sb(name, shape, dt=F32):
            return ctx.enter_context(nc.sbuf_tensor(name, shape, dt))

        def sem(name):
            return ctx.enter_context(nc.semaphore(name))

        x1 = sb("x1", [P, NT, D])
        wcol = sb("wcol2", [P, KC])
        gate = sb("gate", [P, KC, P])
        gs = [sb(f"gate_{n}", [P, KC, P], F32R) for n in ("hi", "lo")]
        low = sb("low", [P, E, E])
        junk = sb("junk", [P, D])
        ms = sb("ms", [P, TT])
        rms, t1, t2 = sb("rms", [P, TT]), sb("rt1", [P, TT]), sb("rt2", [P, TT])
        hn = sb("hn2", [P, TT, D])
        lt = sb("lt", [P, S])
        logits = sb("logits", [P, NT, E])
        top, den = sb("rtop", [P, NT]), sb("den", [P, NT])
        prob, chosen, rank = sb("rprob", [P, NT, E]), sb("chosen", [P, NT, E]), sb("rank", [P, NT, E])
        above, tied = sb("above", [P, NT, E, E]), sb("tied", [P, NT, E, E])
        tr = [ctx.enter_context(nc.psum_tensor(f"tr{i}", [P, S], F32)) for i in range(2)]
        pl = ctx.enter_context(nc.psum_tensor("pl", [P, S], F32))
        plt = ctx.enter_context(nc.psum_tensor("plt", [P, TT, P], F32))
        const_in, x1_in = sem("rconst_in"), sem("x1_in")
        squares, hn_ready, tr_done, tok_hi, tok_lo = sem("squares"), sem("rhn_ready"), sem("rtr_done"), sem("tok_hi"), sem("tok_lo")
        gate_split, logit_done, lt_ready, lt_tr, logit_ready = (sem(n) for n in ("gate_split", "logit_done", "lt_ready", "lt_tr", "logit_ready"))
        shifted, exped, x1_added, own_sem = sem("shifted"), sem("exped"), sem("x1_added"), sem("rown")
        block = ctx.enter_context(nc.Block())

        @block.sync
        def _(sp):
            sp.dma_start(wcol[:, :], w_ffn).then_inc(const_in, 16)
            sp.dma_start(gate[:, :, :], gateT.rearrange("c p e -> p c e")).then_inc(const_in, 16)
            sp.dma_start(low[:, :, :].rearrange("p a b -> p (a b)"), ranklow_d.broadcast_to([P, E * E])).then_inc(const_in, 16)
            sp.dma_start(x1[:, :, :], x1_dram).then_inc(x1_in, 16)

        @block.gpsimd
        def _(pool):
            pool.wait_ge(x1_in, 16)
            with pool.Fori(0, B) as b:
                pool.wait_ge(hn_ready, TT * (b + 1))
                a = acc[:, bass.ds(b * TT, TT), :].rearrange("p t d -> p (t d)")
                nc.gpsimd.tensor_tensor(a, a, x1[:, bass.ds(b * TT, TT), :].rearrange("p t d -> p (t d)"), ALU.add).then_inc(x1_added, 1)
            pool.wait_ge(x1_added, B)

        @block.scalar
        def _(act):
            act.wait_ge(const_in, 48)
            with act.Fori(0, B) as b:
                for t in range(TT):
                    last = nc.scalar.activation(junk[:, :], acc[:, bass.ds(b * TT + t, 1), :].rearrange("p a d -> p (a d)"), ACT.Square,
                                                accum_out=ms[:, t:t + 1])
                    last.then_inc(squares, 1)
                    act.wait_ge(squares, TT * b + t + 1)
                for t in range(TT):
                    act.wait_ge(tr_done, TT * b + t + 1)
                    for k in range(KC):
                        last = nc.scalar.activation(tokT[0][:, k, bass.ds(b * S + t * P, P)], tr[t % 2][:, k * P:(k + 1) * P], ACT.Copy,
                                                    scale=wcol[:, k:k + 1])
                    last.then_inc(tok_hi, 1)
                act.wait_ge(logit_done, b + 1)
                nc.scalar.activation(lt[:, :], pl[:, :], ACT.Copy).then_inc(lt_ready, 1)
            act.wait_ge(shifted, 1)
            nc.scalar.activation(prob[:, :, :], logits[:, :, :], ACT.Exp).then_inc(exped, 1)

        @block.tensor
        def _(pe):
            pe.wait_ge(gate_split, 2)
            with pe.Fori(0, B) as b:
                for t in range(TT):
                    pe.wait_ge(hn_ready, TT * b + t + 1)
                    if t >= 2:
                        pe.wait_ge(tok_lo, TT * b + t - 1)
                    for k in range(KC):
                        last = nc.tensor.transpose(tr[t % 2][:, k * P:(k + 1) * P], hn[:, t, k * P:(k + 1) * P], ident[:, :])
                    last.then_inc(tr_done, 1)
                pe.wait_ge(tok_lo, TT * (b + 1))
                for k in range(KC):
                    for n, (a, c) in enumerate(SPLITS):
                        last = nc.tensor.matmul(pl[:, :], gs[a][:, k, :], tokT[c][:, k, bass.ds(b * S, S)],
                                                start=(k == 0 and n == 0), stop=(k == KC - 1 and n == 2))
                last.then_inc(logit_done, 1)
                pe.wait_ge(lt_ready, b + 1)
                for t in range(TT):
                    last = nc.tensor.transpose(plt[:, t, :], lt[:, t * P:(t + 1) * P], ident[:, :])
                last.then_inc(lt_tr, 1)

        @block.vector
        def _(dve):
            pre = Steps(dve, own_sem)
            dve.wait_ge(const_in, 48)
            nc.vector.tensor_copy(gs[0][:, :, :], gate[:, :, :]).then_inc(gate_split, 1)
            dve.wait_ge(gate_split, 1)
            nc.vector.tensor_tensor(gs[1][:, :, :], gate[:, :, :], gs[0][:, :, :].bitcast(F32), ALU.subtract).then_inc(gate_split, 1)
            with dve.Fori(0, B) as b:
                own = Steps(dve, own_sem, pre.n + b * ROUTER_STEPS)
                dve.wait_ge(squares, TT * (b + 1))
                own.chain(nc.vector.tensor_scalar(ms[:, :], ms[:, :], 1.0 / D, 1e-6, ALU.mult, ALU.add))
                rsqrt(nc, own.chain, rms[:, :], ms[:, :], t1[:, :], t2[:, :])
                for t in range(TT):
                    nc.vector.tensor_scalar(hn[:, t, :], acc[:, bass.ds(b * TT + t, 1), :].rearrange("p a d -> p (a d)"), rms[:, t:t + 1],
                                            None, ALU.mult).then_inc(hn_ready, 1)
                for t in range(TT):
                    dve.wait_ge(tok_hi, TT * b + t + 1)
                    for k in range(KC):
                        last = nc.vector.scalar_tensor_tensor(tokT[1][:, k, bass.ds(b * S + t * P, P)], tr[t % 2][:, k * P:(k + 1) * P],
                                                              wcol[:, k:k + 1], tokT[0][:, k, bass.ds(b * S + t * P, P)].bitcast(F32),
                                                              ALU.mult, ALU.subtract)
                    last.then_inc(tok_lo, 1)
                dve.wait_ge(lt_tr, b + 1)
                nc.vector.tensor_copy(logits[:, bass.ds(b * TT, TT), :], plt[:, :, 0:E]).then_inc(logit_ready, 1)
                assert own.n == ROUTER_STEPS, own.n
            dve.wait_ge(logit_ready, B)
            end = Steps(dve, own_sem, pre.n + B * ROUTER_STEPS)
            row = [P, NT, E]
            end.chain(nc.vector.tensor_reduce(top[:, :], logits[:, :, :], AX.X, ALU.max))
            nc.vector.tensor_tensor(logits[:, :, :], logits[:, :, :], top[:, :].unsqueeze(2).broadcast_to(row), ALU.subtract).then_inc(shifted, 1)
            dve.wait_ge(exped, 1)
            end.chain(nc.vector.tensor_reduce(den[:, :], prob[:, :, :], AX.X, ALU.add))
            end.chain(nc.vector.reciprocal(top[:, :], den[:, :]))
            end.chain(nc.vector.tensor_tensor(prob[:, :, :], prob[:, :, :], top[:, :].unsqueeze(2).broadcast_to(row), ALU.mult))
            pair = [P, NT, E, E]
            other, mine = prob[:, :, :].unsqueeze(2).broadcast_to(pair), prob[:, :, :].unsqueeze(3).broadcast_to(pair)
            end.done(nc.vector.tensor_tensor(above[:, :, :, :], other, mine, ALU.is_gt))
            end.chain(nc.vector.tensor_tensor(tied[:, :, :, :], other, mine, ALU.is_equal))
            end.chain(nc.vector.tensor_tensor(tied[:, :, :, :], tied[:, :, :, :], low[:, :, :].unsqueeze(1).broadcast_to(pair), ALU.mult))
            end.chain(nc.vector.tensor_tensor(above[:, :, :, :], above[:, :, :, :], tied[:, :, :, :], ALU.add))
            end.chain(nc.vector.tensor_reduce(rank[:, :, :], above[:, :, :, :], AX.X, ALU.add))
            end.chain(nc.vector.tensor_scalar(chosen[:, :, :], rank[:, :, :], 1.5, None, ALU.is_lt))
            end.chain(nc.vector.tensor_tensor(chosen[:, :, :], chosen[:, :, :], prob[:, :, :], ALU.mult))
            end.chain(nc.vector.tensor_reduce(den[:, :], chosen[:, :, :], AX.X, ALU.add))
            end.chain(nc.vector.tensor_scalar(den[:, :], den[:, :], 1e-9, None, ALU.add))
            end.chain(nc.vector.reciprocal(top[:, :], den[:, :]))
            end.chain(nc.vector.tensor_tensor(combine[:, :, :], chosen[:, :, :], top[:, :].unsqueeze(2).broadcast_to(row), ALU.mult))


ROUTER_STEPS = 12
CW = 768
NCW = 6


def experts(nc, wexp, acc, tokT, combine, out):
    with ExitStack() as ctx:
        def sb(name, shape, dt=F32):
            return ctx.enter_context(nc.sbuf_tensor(name, shape, dt))

        def sem(name):
            return ctx.enter_context(nc.semaphore(name))

        stage = [sb(f"wstage{i}", [P, CW]) for i in range(2)]
        w = [[sb(f"we{i}_{n}", [P, NCW * CW], F32R) for n in ("hi", "lo")] for i in range(2)]
        gated = [sb(f"gated{i}", [P, S]) for i in range(2)]
        h = [[sb(f"h{i}_{n}", [P, IC, S], F32R) for n in ("hi", "lo")] for i in range(2)]
        bank = [ctx.enter_context(nc.psum_tensor(f"ebank{i}", [P, S], F32)) for i in range(8)]
        DOWN = 4
        stage_in = [sem(f"wstage_in{i}") for i in range(2)]
        passed = sem("passed3")
        w_hi, w_split, up_done, silu_done, gate_done = sem("we_hi"), sem("we_split"), sem("up_done"), sem("silu_done"), sem("gate_done")
        h_hi, h_lo, down_done, added, stored = sem("h_hi"), sem("h_lo"), sem("down_done"), sem("added"), sem("stored")
        FREE = {w_split: 2, gate_done: 2, h_lo: 2, down_done: 17, added: 4}
        STEPS = 2 * B
        block = ctx.enter_context(nc.Block())

        def wgu(eh, part, up, k, c):
            at = up * KC * IP + k * IP + c * P
            return w[eh][part][:, at:at + P]

        def wdown(eh, part, c):
            at = 2 * KC * IP + c * D
            return w[eh][part][:, at:at + D]

        @block.sync
        def _(sp):
            with sp.Fori(0, E // 2) as g:
                for i in range(2 * NCW):
                    sp.wait_ge(w_split, FREE[w_split] + 2 * NCW * g + i - 1)
                    sp.dma_start(stage[i % 2][:, :], wexp[bass.ds(2 * g + i // NCW, 1), i % NCW, :, :].rearrange("g p n -> (g p) n")
                                 ).then_inc(stage_in[i % 2], 16)
            for b in range(B):
                sp.wait_ge(added, FREE[added] + TT * ((E - 1) * B + b + 1))
                sp.dma_start(out[b * S:(b + 1) * S, :].rearrange("(t p) d -> p t d", p=P), acc[:, b * TT:(b + 1) * TT, :]).then_inc(stored, 16)
            sp.wait_ge(stored, 16 * B)

        @block.gpsimd
        def _(pool):
            with pool.Fori(0, E // 2) as g:
                for i in range(2 * NCW):
                    eh, c = i // NCW, i % NCW
                    if c == 0:
                        pool.wait_ge(down_done, FREE[down_done] + 16 * (2 * g + eh) - 16)
                    wait_apart(pool, passed, stage_in[i % 2], 16 * (NCW * g + i // 2 + 1))
                    sl = slice(c * CW, (c + 1) * CW)
                    nc.gpsimd.tensor_copy(w[eh][0][:, sl], stage[i % 2][:, :]).then_inc(w_hi, 1)
                    pool.wait_ge(w_hi, 2 * NCW * g + i + 1)
                    nc.gpsimd.tensor_tensor(w[eh][1][:, sl], stage[i % 2][:, :], w[eh][0][:, sl].bitcast(F32), ALU.subtract).then_inc(w_split, 1)

        @block.tensor
        def _(pe):
            def up(g, n, c):
                eh, b = n // B, n % B
                k0 = IC * n + c
                if b == 0 and c == 0:
                    pe.wait_ge(w_split, FREE[w_split] + NCW * (2 * g + eh + 1))
                pe.wait_ge(gate_done, FREE[gate_done] + IC * STEPS * g + k0 - 1)
                for u in range(2):
                    for k in range(KC):
                        for i, (a, m) in enumerate(SPLITS):
                            last = nc.tensor.matmul(bank[2 * (k0 % 2) + u][:, :], wgu(eh, a, u, k, c), tokT[m][:, k, b * S:(b + 1) * S],
                                                    start=(k == 0 and i == 0), stop=(k == KC - 1 and i == 2))
                last.then_inc(up_done, 1)

            def down(g, n, t):
                eh = n // B
                if t == 0:
                    pe.wait_ge(h_lo, FREE[h_lo] + IC * (STEPS * g + n + 1))
                pe.wait_ge(added, FREE[added] + TT * (STEPS * g + n) + t - 3)
                for c in range(IC):
                    for i, (a, m) in enumerate(SPLITS):
                        last = nc.tensor.matmul(bank[DOWN + t][:, :], h[n % 2][a][:, c, t * P:(t + 1) * P], wdown(eh, m, c),
                                                start=(c == 0 and i == 0), stop=(c == IC - 1 and i == 2))
                last.then_inc(down_done, 1)

            pe.sem_inc(down_done, FREE[down_done])
            with pe.Fori(0, E // 2) as g:
                for n in range(STEPS):
                    for c, downs in enumerate(((0,), (1, 2), (3,))):
                        up(g, n, c)
                        if n:
                            for t in downs:
                                down(g, n - 1, t)
                for t in range(TT):
                    down(g, STEPS - 1, t)

        @block.scalar
        def _(act):
            with act.Fori(0, E // 2) as g:
                for n in range(STEPS):
                    for c in range(IC):
                        k0 = IC * n + c
                        act.wait_ge(up_done, IC * STEPS * g + k0 + 1)
                        act.wait_ge(h_lo, FREE[h_lo] + IC * STEPS * g + k0 - 1)
                        nc.scalar.activation(gated[k0 % 2][:, :], bank[2 * (k0 % 2)][:, :], ACT.Silu).then_inc(silu_done, 1)
                        act.wait_ge(gate_done, FREE[gate_done] + IC * STEPS * g + k0 + 1)
                        if c == 0:
                            act.wait_ge(down_done, FREE[down_done] + TT * (STEPS * g + n) - TT)
                        nc.scalar.activation(h[n % 2][0][:, c, :], gated[k0 % 2][:, :], ACT.Copy).then_inc(h_hi, 1)

        @block.vector
        def _(dve):
            def add(g, n, t):
                tile = (n % B) * TT + t
                dve.wait_ge(down_done, FREE[down_done] + TT * (STEPS * g + n) + t + 1)
                nc.vector.scalar_tensor_tensor(acc[:, tile, :], bank[DOWN + t][:, :],
                                               combine[:, tile, bass.ds(2 * g + n // B, 1)], acc[:, tile, :],
                                               ALU.mult, ALU.add).then_inc(added, 1)

            for s in (w_split, gate_done, h_lo, added):
                dve.sem_inc(s, FREE[s])
            with dve.Fori(0, E // 2) as g:
                for n in range(STEPS):
                    for c, downs in enumerate(((0,), (1, 2), (3,))):
                        k0 = IC * n + c
                        o = gated[k0 % 2]
                        dve.wait_ge(silu_done, IC * STEPS * g + k0 + 1)
                        nc.vector.tensor_tensor(o[:, :], bank[2 * (k0 % 2) + 1][:, :], o[:, :], ALU.mult).then_inc(gate_done, 1)
                        dve.wait_ge(h_hi, IC * STEPS * g + k0 + 1)
                        nc.vector.tensor_tensor(h[n % 2][1][:, c, :], o[:, :], h[n % 2][0][:, c, :].bitcast(F32), ALU.subtract).then_inc(h_lo, 1)
                        if n:
                            for t in downs:
                                add(g, n - 1, t)
                for t in range(TT):
                    add(g, STEPS - 1, t)


def kernel(x, ctx_2048, L0_ffn_attn_norm_w, L0_ffn_q_w, L0_ffn_k_w, L0_ffn_v_w, L0_ffn_o_w, L0_ffn_q_norm_w, L0_ffn_k_norm_w,
           L0_ffn_ffn_norm_w, L0_ffn_gate_w, L0_ffn_wg, L0_ffn_wu, L0_ffn_wd):
    import numpy as np
    import concourse.bacc as bacc
    from concourse.bass_utils import run_bass_kernel_spmd

    f = np.float32
    qT = np.asarray(L0_ffn_q_w).reshape(HKV, G * HD, D).transpose(0, 2, 1)
    kT = np.asarray(L0_ffn_k_w).reshape(HKV, HD, D).transpose(0, 2, 1)
    vT = np.asarray(L0_ffn_v_w).reshape(HKV, HD, D).transpose(0, 2, 1)
    oT = np.asarray(L0_ffn_o_w).T.reshape(HKV, G, HD, D)
    wqkvo = np.zeros((HKV + 1, 10, P, 512), f)
    wqkvo[:HKV, 0:4] = qT.reshape(HKV, KC, P, 512)
    kv = np.concatenate([kT, vT], axis=2).reshape(HKV, 2, 2, P, 2 * HD)
    wqkvo[:HKV, 4:6] = kv.transpose(0, 1, 3, 2, 4).reshape(HKV, 2, P, 512)
    wqkvo[:HKV, 6:10] = oT
    wexp = np.zeros((E, NCW, P, CW), f)
    for n, a in enumerate((L0_ffn_wg, L0_ffn_wu)):
        padded = np.zeros((E, D, IP), f)
        padded[:, :, :I] = np.asarray(a).transpose(0, 2, 1)
        padded = padded.reshape(E, KC, P, IP).transpose(0, 2, 1, 3).reshape(E, P, 2, CW)
        wexp[:, 2 * n:2 * n + 2] = padded.transpose(0, 2, 1, 3)
    padded = np.zeros((E, IP, D), f)
    padded[:, :I] = np.asarray(L0_ffn_wd).transpose(0, 2, 1)
    padded = padded.reshape(E, IC, P, D).transpose(0, 2, 1, 3).reshape(E, P, 2, CW)
    wexp[:, 4:6] = padded.transpose(0, 2, 1, 3)
    gateT = np.zeros((KC, P, P), f)
    gateT[:, :, :E] = np.asarray(L0_ffn_gate_w).T.reshape(KC, P, E)
    freqs = (f(1.0) / np.power(f(1000000.0), np.arange(0, HD, 2, dtype=f) / f(HD), dtype=f)).astype(f)
    angle = np.outer(np.arange(S, dtype=f), freqs).astype(f)
    tables = [t.astype(f).reshape(TT, P, HD // 2).transpose(1, 0, 2).reshape(P, TT * HD // 2) for t in (np.cos(angle), np.sin(angle))]
    mask = np.where(np.arange(P)[None, :] > np.arange(P)[:, None], f(-1e30), f(0.0)).astype(f)
    low = (np.arange(E)[None, :] < np.arange(E)[:, None]).astype(f).reshape(1, E * E)
    arrays = {
        "x": np.asarray(x).reshape(B * S, D), "ctxT": np.asarray(ctx_2048).transpose(0, 2, 1), "w_attn": np.asarray(L0_ffn_attn_norm_w).reshape(KC, P).T,
        "wqkvo": wqkvo, "qn": np.asarray(L0_ffn_q_norm_w), "kn": np.asarray(L0_ffn_k_norm_w), "cos": tables[0], "sin": tables[1],
        "w_ffn": np.asarray(L0_ffn_ffn_norm_w).reshape(KC, P).T, "gateT": gateT, "wexp": wexp, "ident": np.eye(P, dtype=f), "mask": mask, "ranklow": low,
    }
    arrays = {f"in_{n}": np.ascontiguousarray(a) for n, a in arrays.items()}
    nc = bacc.Bacc("TRN2", target_bir_lowering=False, num_devices=1)
    args = [nc.dram_tensor(n, a.shape, mybir.dt.from_np(a.dtype), kind="ExternalInput").ap() for n, a in arrays.items()]
    out = nc.dram_tensor("out", (B * S, D), F32, kind="ExternalOutput").ap()
    build(nc, *args, out)
    r = run_bass_kernel_spmd(nc, [arrays], core_ids=[0])
    return r.results[0]["out"].reshape(B, S, D)
```

```python
import concourse.bass as bass
from concourse import mybir
from contextlib import ExitStack

F32 = mybir.dt.float32
F32R = mybir.dt.float32r
BF16 = mybir.dt.bfloat16
U32 = mybir.dt.uint32
I32 = mybir.dt.int32
ALU = mybir.AluOpType
ACT = mybir.ActivationFunctionType
AX = mybir.AxisListType

B, S, D = 4, 512, 512
P = 128
NT = B * S // P
TT = S // P
KC = D // P
HD = 128
HQ, HKV = 16, 4
G = HQ // HKV
E, I = 8, 352
IC = -(-I // P)
IP = IC * P
CH = 512
RING = 5
FP8_MAX = 448.0
RSQRT_MAGIC = float(0x5F3759DF)
EXPONENT_BITS = 0x7F800000
FP8_LEAST_NORMAL = 2.0 ** -6
FP8_ROUND = 1.5 * 2.0 ** 20
SPLITS = ((0, 0), (0, 1), (1, 0))


class Steps:

    def __init__(self, engine, sem, base=0):
        self.engine, self.sem, self.base, self.n = engine, sem, base, 0

    def done(self, ins):
        self.n += 1
        ins.then_inc(self.sem, 1)

    def wait(self):
        self.engine.wait_ge(self.sem, self.base + self.n)

    def chain(self, ins):
        self.done(ins)
        self.wait()


def wait_apart(engine, passed, sem, value):
    engine.wait_ge(sem, value)
    engine.sem_inc(passed, 1)


def rsqrt(nc, chain, out, x, t, u):
    chain(nc.vector.tensor_scalar(u.bitcast(U32), x.bitcast(U32), 1, None, ALU.logical_shift_right))
    chain(nc.vector.tensor_scalar(out.bitcast(I32), u.bitcast(I32), -1.0, RSQRT_MAGIC, ALU.mult, ALU.add))
    for _ in range(3):
        chain(nc.vector.tensor_tensor(t, out, out, ALU.mult))
        chain(nc.vector.scalar_tensor_tensor(u, t, -0.5, x, ALU.mult, ALU.mult))
        chain(nc.vector.scalar_tensor_tensor(out, u, 1.5, out, ALU.add, ALU.mult))


def build(nc, x, ctxT, w_attn, wqkvo, qn, kn, cos, sin, w_ffn, gateT, wexp, ident_d, mask_d, ranklow_d, out):
    ctx = ExitStack()
    with ctx:
        acc = ctx.enter_context(nc.sbuf_tensor("acc", [P, NT, D], F32))
        ident = ctx.enter_context(nc.sbuf_tensor("ident", [P, P], F32))
        identb = ctx.enter_context(nc.sbuf_tensor("identb", [P, P], BF16))
        x1_dram = nc.dram_tensor("x1_scratch", (P, NT, D), F32, kind="Internal").ap()
        hT_dram = nc.dram_tensor("hT_scratch", (B, P, 2 * KC * S), F32, kind="Internal").ap()
        with ExitStack() as ahead:
            stage = [ahead.enter_context(nc.sbuf_tensor(f"stage{i}", [P, CH], F32)) for i in range(RING)]
            tab = {(n, f): ahead.enter_context(nc.sbuf_tensor(f"tab_{n}_{f}", [P, TT, HD], F32)) for n in "qk" for f in "cs"}
            mask = ahead.enter_context(nc.sbuf_tensor("mask", [P, P], BF16))
            quant_projection(nc, x, ctxT, w_attn, ident_d, wqkvo, qn, kn, cos, sin, mask_d, acc, ident, identb, stage, tab, mask,
                             x1_dram, hT_dram)
            attention(nc, wqkvo, acc, ident, identb, stage, tab, mask, hT_dram)
        with ExitStack() as moe:
            tokT = [moe.enter_context(nc.sbuf_tensor(f"tokT_{n}", [P, KC, B * S], F32R)) for n in ("hi", "lo")]
            combine = moe.enter_context(nc.sbuf_tensor("combine", [P, NT, E], F32))
            router(nc, w_ffn, gateT, ranklow_d, acc, ident, tokT, combine, x1_dram)
            experts(nc, wexp, acc, tokT, combine, out)


def quant_projection(nc, x, ctxT, w_attn, ident_d, wqkvo, qn, kn, cos, sin, mask_d, acc, ident, identb, stage, tab, mask,
                     x1_dram, hT_dram):
    with ExitStack() as ctx:
        def sb(name, shape, dt=F32):
            return ctx.enter_context(nc.sbuf_tensor(name, shape, dt))

        def sem(name):
            return ctx.enter_context(nc.semaphore(name))

        H = HD // 2
        wrow = {n: sb(f"wrow_{n}", [P, HD]) for n in "qk"}
        wneg = {n: sb(f"wneg_{n}", [P, H]) for n in "qk"}
        zero = sb("zero", [P, H])
        cos_sb, sin_sb = sb("cos_sb", [P, TT * H]), sb("sin_sb", [P, TT * H])
        mask_sb = sb("mask_sb", [P, P])
        xs = sb("xs", [P, NT, D])
        cs = sb("cs", [P, B * KC, S])
        wcol = sb("wcol", [P, KC])
        camax = sb("camax", [P, B * KC * 4])
        camaxall = sb("camaxall", [P, B * KC * 4])
        cinv = sb("cinv", [P, B * KC * 4])
        cscale = sb("cscale", [P, B * KC * 4])
        cv = sb("cv", [P, KC * S])
        cm = sb("cm", [P, KC * S])
        cq = sb("cq", [P, B * KC, S], BF16)
        stats = sb("stats", [P, TT, 6])
        mv = sb("mv", [P, TT, 2])
        var = sb("var", [P, TT])
        rstd = sb("rstd", [P, TT])
        t1 = sb("t1", [P, TT])
        t2 = sb("t2", [P, TT])
        xhat = sb("xhat", [P, TT, D])
        amax = sb("amax", [P, TT * KC])
        ainv = sb("ainv", [P, TT * KC])
        ascale = sb("ascale", [P, NT * KC])
        comb = sb("comb", [P, TT, KC, 4])
        v = sb("v", [P, TT, D])
        m = sb("m", [P, TT, D])
        xq = sb("xq", [P, TT, D], BF16)
        xqT = sb("xqT", [P, TT, KC, P], BF16)
        hn = xhat
        hT = [sb(f"hT_{n}", [P, KC, S], F32R) for n in ("hi", "lo")]
        part = [ctx.enter_context(nc.psum_tensor(f"part{i}", [P, S], F32)) for i in range(KC)]
        trq = [ctx.enter_context(nc.psum_tensor(f"trq{i}", [P, KC, P], BF16)) for i in range(2)]
        trh = [ctx.enter_context(nc.psum_tensor(f"trh{i}", [P, S], F32)) for i in range(2)]

        const_in, ctx_in, x_in = sem("const_in"), [sem(f"ctx_in{i}") for i in range(B)], [sem(f"x_in{i}") for i in range(B)]
        identb_ready, ctx_colmax, ctx_max = sem("identb_ready"), sem("ctx_colmax"), sem("ctx_max")
        passed = sem("passed1")
        dve_step, pool_step = sem("dve_step"), sem("pool_step")
        ctx_magic, ctx_quant = sem("ctx_magic"), sem("ctx_quant")
        xhat_ready, v_ready, magic_ready, xq_ready = sem("xhat_ready"), sem("v_ready"), sem("magic_ready"), sem("xq_ready")
        trq_done, xqT_ready, part_done, part_used = sem("trq_done"), sem("xqT_ready"), sem("part_done"), sem("part_used")
        x1_ready, hn_ready, trh_done, hi_ready, lo_ready = (sem(n) for n in ("x1_ready", "hn_ready", "trh_done", "hi_ready", "lo_ready"))
        x1_saved, hT_saved = sem("x1_saved"), sem("hT_saved")
        table_in, ahead_in, table_step = sem("table_in"), sem("ahead_in"), sem("table_step")
        block = ctx.enter_context(nc.Block())

        @block.sync
        def _(sp):
            def load_x(b):
                sp.dma_start(xs[:, b * TT:(b + 1) * TT, :],
                             x[b * S:(b + 1) * S, :].rearrange("(t p) d -> p t d", p=P)).then_inc(x_in[b], 16)

            load_x(0)
            for b in range(B):
                sp.dma_start(cs[:, b * KC:(b + 1) * KC, :], ctxT[b].rearrange("(c p) n -> p c n", p=P)).then_inc(ctx_in[b], 16)
            for b in range(1, B):
                load_x(b)
            for n, norm in (("q", qn), ("k", kn)):
                sp.dma_start(wrow[n][:, :], norm.rearrange("(a d) -> a d", a=1).broadcast_to([P, HD])).then_inc(table_in, 16)
            sp.dma_start(cos_sb[:, :], cos).then_inc(table_in, 16)
            sp.dma_start(sin_sb[:, :], sin).then_inc(table_in, 16)
            sp.dma_start(mask_sb[:, :], mask_d).then_inc(table_in, 16)
            for c in range(RING):
                sp.dma_start(stage[c][:, :], wqkvo[0, c, :, :]).then_inc(ahead_in, 16)
            with sp.Fori(0, B) as b:
                sp.wait_ge(x1_ready, b + 1)
                sp.dma_start(x1_dram[:, bass.ds(b * TT, TT), :], xs[:, bass.ds(b * TT, TT), :]).then_inc(x1_saved, 16)
                sp.wait_ge(lo_ready, TT * (b + 1))
                for i in range(2):
                    sp.dma_start(hT_dram[bass.ds(b, 1), :, i * KC * S:(i + 1) * KC * S].rearrange("b p n -> (b p) n"),
                                 hT[i][:, :, :].rearrange("p c n -> p (c n)").bitcast(F32)).then_inc(hT_saved, 16)
            sp.wait_ge(ahead_in, 16 * RING)
            sp.wait_ge(x1_saved, 16 * B)
            sp.wait_ge(hT_saved, 32 * (B + 1))

        @block.scalar
        def _(act):
            act.dma_start(wcol[:, :], w_attn).then_inc(const_in, 16)
            act.dma_start(ident[:, :], ident_d).then_inc(const_in, 16)
            act.wait_ge(const_in, 32)
            nc.scalar.activation(identb[:, :], ident[:, :], ACT.Copy).then_inc(identb_ready, 1)

            def scale_rows(b):
                act.wait_ge(xhat_ready, b + 1)
                if not isinstance(b, int):
                    act.wait_ge(xq_ready, TT * b)
                for t in range(TT):
                    for k in range(KC):
                        last = nc.scalar.activation(v[:, t, k * P:(k + 1) * P], xhat[:, t, k * P:(k + 1) * P], ACT.Copy,
                                                    scale=ainv[:, t * KC + k:t * KC + k + 1])
                    last.then_inc(v_ready, 1)

            def copy_xqT(b):
                for t in range(TT):
                    act.wait_ge(trq_done, TT * b + t + 1)
                    nc.scalar.activation(xqT[:, t, :, :], trq[t % 2][:, :, :], ACT.Copy).then_inc(xqT_ready, 1)

            def hi_h(b):
                act.wait_ge(hT_saved, 32 * (b + 1))
                for t in range(TT):
                    act.wait_ge(trh_done, TT * b + t + 1)
                    for k in range(KC):
                        last = nc.scalar.activation(hT[0][:, k, t * P:(t + 1) * P], trh[t % 2][:, k * P:(k + 1) * P],
                                                    ACT.Copy, scale=wcol[:, k:k + 1])
                    last.then_inc(hi_ready, 1)

            act.sem_inc(hT_saved, 32)
            scale_rows(0)
            copy_xqT(0)
            with act.Fori(0, B - 1) as b:
                scale_rows(b + 1)
                hi_h(b)
                copy_xqT(b + 1)
            hi_h(B - 1)

        @block.gpsimd
        def _(pool):
            pool.wait_ge(ctx_colmax, 1)
            nc.gpsimd.partition_all_reduce(camaxall[:, :], camax[:, :], P, bass.bass_isa.ReduceOp.max).then_inc(ctx_max, 1)

            def round_fp8(b):
                pool.wait_ge(ctx_magic, b + 1)
                nc.gpsimd.tensor_tensor(cv[:, :], cv[:, :], cm[:, :], ALU.add).then_inc(pool_step, 1)
                pool.wait_ge(pool_step, (TT + 1) * b + 1)
                nc.gpsimd.tensor_tensor(cq[:, bass.ds(b * KC, KC), :].rearrange("p c n -> p (c n)"), cv[:, :], cm[:, :],
                                        ALU.subtract).then_inc(ctx_quant, 1)
                if not isinstance(b, int):
                    pool.wait_ge(trq_done, TT * b)
                for t in range(TT):
                    pool.wait_ge(magic_ready, TT * b + t + 1)
                    nc.gpsimd.tensor_tensor(v[:, t, :], v[:, t, :], m[:, t, :], ALU.add).then_inc(pool_step, 1)
                    pool.wait_ge(pool_step, (TT + 1) * b + t + 2)
                    nc.gpsimd.tensor_tensor(xq[:, t, :], v[:, t, :], m[:, t, :], ALU.subtract).then_inc(xq_ready, 1)

            round_fp8(0)
            with pool.Fori(0, B - 1) as b:
                round_fp8(b + 1)
            pool.wait_ge(table_in, 16 * 5)
            nc.gpsimd.tensor_copy(mask[:, :], mask_sb[:, :])
            nc.gpsimd.memset(zero[:, :], 0.0).then_inc(table_step, 1)
            pool.wait_ge(table_step, 1)
            for n in "qk":
                nc.gpsimd.tensor_tensor(wneg[n][:, :], zero[:, :], wrow[n][:, H:HD], ALU.subtract).then_inc(table_step, 1)
            pool.wait_ge(table_step, 3)
            c3, s3 = cos_sb[:, :].rearrange("p (t h) -> p t h", h=H), sin_sb[:, :].rearrange("p (t h) -> p t h", h=H)
            for n in "qk":
                for a in range(2):
                    sl = slice(a * H, (a + 1) * H)
                    other = wrow[n][:, 0:H] if a else wneg[n][:, :]
                    nc.gpsimd.tensor_tensor(tab[n, "c"][:, :, sl], c3, wrow[n][:, sl].unsqueeze(1).broadcast_to([P, TT, H]), ALU.mult)
                    nc.gpsimd.tensor_tensor(tab[n, "s"][:, :, sl], s3, other.unsqueeze(1).broadcast_to([P, TT, H]), ALU.mult)

        @block.tensor
        def _(pe):
            pe.wait_ge(identb_ready, 1)

            def transpose_rows(b):
                for t in range(TT):
                    pe.wait_ge(xq_ready, TT * b + t + 1)
                    if t >= 2:
                        pe.wait_ge(xqT_ready, TT * b + t - 1)
                    for k in range(KC):
                        last = nc.tensor.transpose(trq[t % 2][:, k, :], xq[:, t, k * P:(k + 1) * P], identb[:, :])
                    last.then_inc(trq_done, 1)

            def products(b):
                pe.wait_ge(ctx_quant, b + 1)
                for t in range(TT):
                    pe.wait_ge(xqT_ready, TT * b + t + 1)
                    for k in range(KC):
                        if t:
                            pe.wait_ge(part_used, TT * KC * b + KC * (t - 1) + k + 1)
                        nc.tensor.matmul(part[k][:, :], xqT[:, t, k, :], cq[:, bass.ds(b * KC + k, 1), :].rearrange("p c n -> p (c n)"),
                                         start=True, stop=True).then_inc(part_done, 1)

            def transpose_h(b):
                for t in range(TT):
                    pe.wait_ge(hn_ready, TT * b + t + 1)
                    if t >= 2:
                        pe.wait_ge(lo_ready, TT * b + t - 1)
                    for k in range(KC):
                        last = nc.tensor.transpose(trh[t % 2][:, k * P:(k + 1) * P], hn[:, t, k * P:(k + 1) * P], ident[:, :])
                    last.then_inc(trh_done, 1)

            transpose_rows(0)
            with pe.Fori(0, B - 1) as b:
                products(b)
                transpose_h(b)
                transpose_rows(b + 1)
            products(B - 1)
            transpose_h(B - 1)

        @block.vector
        def _(dve):
            def moments(own, tile):
                for t in range(TT):
                    own.done(nc.vector.bn_stats(stats[:, t, :], tile(t)))
                wait_apart(dve, passed, dve_step, own.base + own.n)
                for t in range(TT):
                    own.done(nc.vector.bn_aggr(mv[:, t, :], stats[:, t, :]))
                own.wait()

            def normalise_rows(b, own):
                moments(own, lambda t: xs[:, bass.ds(b * TT + t, 1), :].rearrange("p a d -> p (a d)"))
                own.chain(nc.vector.tensor_scalar(var[:, :], mv[:, :, 1], 1e-5, None, ALU.add))
                rsqrt(nc, own.chain, rstd[:, :], var[:, :], t1[:, :], t2[:, :])
                for t in range(TT):
                    own.chain(nc.vector.tensor_scalar(xhat[:, t, :], xs[:, bass.ds(b * TT + t, 1), :].rearrange("p a d -> p (a d)"),
                                                      mv[:, t, 0:1], rstd[:, t:t + 1], ALU.subtract, ALU.mult))
                own.chain(nc.vector.tensor_reduce(amax[:, :], xhat[:, :, :].rearrange("p t (k d) -> p (t k) d", d=P), AX.X, ALU.max,
                                                  apply_absolute_value=True))
                own.chain(nc.vector.tensor_scalar(amax[:, :], amax[:, :], 1e-4, None, ALU.max))
                own.chain(nc.vector.reciprocal(ainv[:, :], amax[:, :]))
                nc.vector.tensor_scalar(ainv[:, :], ainv[:, :], FP8_MAX, None, ALU.mult).then_inc(xhat_ready, 1)
                own.chain(nc.vector.tensor_scalar(ascale[:, bass.ds(b * TT * KC, TT * KC)], amax[:, :], 1.0 / FP8_MAX, None, ALU.mult))

            def scale_ctx(b, own):
                if not isinstance(b, int):
                    dve.wait_ge(ctx_quant, b)
                cblock = cs[:, bass.ds(b * KC, KC), :].rearrange("p c (n k) -> p (c n) k", k=P)
                own.chain(nc.vector.tensor_tensor(cv[:, :].rearrange("p (a k) -> p a k", k=P), cblock,
                                                  cinv[:, bass.ds(b * 16, 16)].unsqueeze(2).broadcast_to([P, 16, P]), ALU.mult))
                own.chain(nc.vector.tensor_scalar(cm[:, :].bitcast(U32), cv[:, :].bitcast(U32), EXPONENT_BITS, None, ALU.bitwise_and))
                nc.vector.tensor_scalar(cm[:, :], cm[:, :], FP8_LEAST_NORMAL, FP8_ROUND, ALU.max, ALU.mult).then_inc(ctx_magic, 1)

            def magic_rows(b, own):
                for t in range(TT):
                    dve.wait_ge(v_ready, TT * b + t + 1)
                    own.chain(nc.vector.tensor_scalar(m[:, t, :].bitcast(U32), v[:, t, :].bitcast(U32), EXPONENT_BITS, None, ALU.bitwise_and))
                    nc.vector.tensor_scalar(m[:, t, :], m[:, t, :], FP8_LEAST_NORMAL, FP8_ROUND, ALU.max, ALU.mult).then_inc(magic_ready, 1)

            def sum_and_norms(b, own, between):
                for t in range(TT):
                    own.done(nc.vector.tensor_tensor(comb[:, t, :, :], cscale[:, bass.ds(b * 16, 16)].rearrange("p (k n) -> p k n", n=4),
                                                     ascale[:, bass.ds(b * TT * KC + t * KC, KC)].unsqueeze(2).broadcast_to([P, KC, 4]), ALU.mult))
                own.wait()
                for t in range(TT):
                    for k in range(KC):
                        dve.wait_ge(part_done, TT * KC * b + KC * t + k + 1)
                        if k:
                            dve.wait_ge(part_used, TT * KC * b + KC * t + k)
                        for n in range(4):
                            x1 = xs[:, bass.ds(b * TT + t, 1), n * P:(n + 1) * P].rearrange("p a d -> p (a d)")
                            last = nc.vector.scalar_tensor_tensor(x1, part[k][:, n * P:(n + 1) * P], comb[:, t, k, n:n + 1], x1,
                                                                  ALU.mult, ALU.add)
                        last.then_inc(part_used, 1)
                between()
                wait_apart(dve, passed, part_used, TT * KC * (b + 1))
                moments(own, lambda t: xs[:, bass.ds(b * TT + t, 1), :].rearrange("p a d -> p (a d)"))
                own.chain(nc.vector.tensor_scalar(var[:, :], mv[:, :, 1], 1e-5, None, ALU.add))
                rsqrt(nc, own.chain, rstd[:, :], var[:, :], t1[:, :], t2[:, :])
                for t in range(TT):
                    own.done(nc.vector.tensor_scalar(acc[:, bass.ds(b * TT + t, 1), :].rearrange("p a d -> p (a d)"),
                                                     xs[:, bass.ds(b * TT + t, 1), :].rearrange("p a d -> p (a d)"),
                                                     mv[:, t, 0:1], rstd[:, t:t + 1], ALU.subtract, ALU.mult))
                own.chain(nc.vector.tensor_tensor(t1[:, :], rstd[:, :], rstd[:, :], ALU.mult))
                own.chain(nc.vector.tensor_tensor(var[:, :], t1[:, :], mv[:, :, 1], ALU.mult))
                nc.vector.tensor_scalar(var[:, :], var[:, :], 1e-6, None, ALU.add).then_inc(x1_ready, 1)
                dve.wait_ge(x1_ready, b + 1)
                rsqrt(nc, own.chain, rstd[:, :], var[:, :], t1[:, :], t2[:, :])
                for t in range(TT):
                    nc.vector.tensor_scalar(hn[:, t, :], acc[:, bass.ds(b * TT + t, 1), :].rearrange("p a d -> p (a d)"),
                                            rstd[:, t:t + 1], None, ALU.mult).then_inc(hn_ready, 1)
                for t in range(TT):
                    dve.wait_ge(hi_ready, TT * b + t + 1)
                    for k in range(KC):
                        last = nc.vector.scalar_tensor_tensor(hT[1][:, k, t * P:(t + 1) * P], trh[t % 2][:, k * P:(k + 1) * P],
                                                              wcol[:, k:k + 1], hT[0][:, k, t * P:(t + 1) * P].bitcast(F32),
                                                              ALU.mult, ALU.subtract)
                    last.then_inc(lo_ready, 1)

            pre = Steps(dve, dve_step)
            dve.wait_ge(x_in[0], 16)
            normalise_rows(0, pre)
            for b in range(B):
                dve.wait_ge(ctx_in[b], 16)
                last = nc.vector.tensor_reduce(camax[:, b * 16:(b + 1) * 16],
                                               cs[:, b * KC:(b + 1) * KC, :].rearrange("p c (n k) -> p (c n) k", k=P),
                                               AX.X, ALU.max, apply_absolute_value=True)
            last.then_inc(ctx_colmax, 1)
            dve.wait_ge(ctx_max, 1)
            pre.chain(nc.vector.tensor_scalar(camax[:, :], camaxall[:, :], 1e-6, None, ALU.max))
            pre.chain(nc.vector.reciprocal(cinv[:, :], camax[:, :]))
            pre.chain(nc.vector.tensor_scalar(cinv[:, :], cinv[:, :], FP8_MAX, None, ALU.mult))
            pre.chain(nc.vector.tensor_scalar(cscale[:, :], camax[:, :], 1.0 / FP8_MAX, None, ALU.mult))
            scale_ctx(0, pre)
            magic_rows(0, pre)
            for b in range(1, B):
                dve.wait_ge(x_in[b], 16)
            dve.wait_ge(const_in, 32)
            with dve.Fori(0, B - 1) as b:
                own = Steps(dve, dve_step, pre.n + b * LOOP1_STEPS)
                normalise_rows(b + 1, own)
                scale_ctx(b + 1, own)
                sum_and_norms(b, own, lambda: magic_rows(b + 1, own))
                assert own.n == LOOP1_STEPS, own.n
            sum_and_norms(B - 1, Steps(dve, dve_step, pre.n + (B - 1) * LOOP1_STEPS), lambda: None)


LOOP1_STEPS = 75


FILL = {(0, 1): [("u", 4)], (0, 2): [("q", 0)], (0, 3): [("kv", 0), ("q", 1)],
        (1, 1): [("kv", 1)], (1, 2): [("q", 2)], (1, 3): [("kv", 2)],
        (2, 1): [("q", 3)], (2, 2): [("kv", 3)], (2, 3): [("n", 0), ("o", 0)],
        (3, 1): [("m", 0), ("o", 1)], (3, 2): [("o", 2)], (3, 3): [("t", 0), ("t", 1), ("t", 2), ("o", 3), ("t", 3)]}


def attention(nc, wqkvo, acc, ident, identb, stage, tab, mask, hT_dram):
    with ExitStack() as ctx:
        def sb(name, shape, dt=F32):
            return ctx.enter_context(nc.sbuf_tensor(name, shape, dt))

        def sem(name):
            return ctx.enter_context(nc.semaphore(name))

        NCH, QKV = 10, 6
        R = G * HD + HD
        KEYS = [(q + 1) * P for q in range(TT)]
        P_AT = [sum(KEYS[:q]) for q in range(TT)]
        QS = [S - j * P for j in range(TT)]
        PT_AT = [sum(QS[:j]) for j in range(TT)]

        hT = sb("hTb", [P, 2, KC, S], F32R)
        w = [sb(f"w_{n}", [P, NCH * CH], F32R) for n in ("hi", "lo")]
        rot = [sb(f"rot{i}", [P, R]) for i in range(2)]
        r = sb("r", [P, TT, R])
        qT = [sb(f"qT_{n}", [P, G, S], F32R) for n in ("hi", "lo")]
        kT = [[sb(f"kT{i}_{n}", [P, S], F32R) for n in ("hi", "lo")] for i in range(2)]
        v = [[sb(f"v{i}_{n}", [P, TT, HD], F32R) for n in ("hi", "lo")] for i in range(2)]
        prob = [sb(f"prob{i}", [P, sum(KEYS)]) for i in range(2)]
        pT = [sb(f"pT_{n}", [P, sum(QS)], F32R) for n in ("hi", "lo")]
        aT = [[sb(f"aT{i}_{n}", [P, G, S], F32R) for n in ("hi", "lo")] for i in range(2)]
        ssum = sb("ssum", [P, TT, G + 1])
        rn = sb("rn", [P, TT, G + 1])
        n1, n2, n15 = (sb(n, [P, TT * (G + 1)]) for n in ("n1", "n2", "n15"))
        scale = [sb(f"scale{i}", [P, TT, G]) for i in range(2)]
        nscale = [sb(f"nscale{i}", [P, TT, G]) for i in range(2)]
        top, bias = sb("top", [P, G * TT]), sb("bias", [P, G * TT])
        total, rtotal = sb("total", [P, G * TT]), sb("rtotal", [P, G * TT])
        bank = [ctx.enter_context(nc.psum_tensor(f"bank{i}", [P, S], F32)) for i in range(8)]
        SC, PT, PV = 3, 5, 7
        TR = (PT, PT + 1, 2, PT, 2)

        ht_in = sem("ht_in")
        stage_in = [sem(f"stage_in{i}") for i in range(RING)]
        w_hi, w_split = sem("w_hi"), sem("w_split")
        projq, projkv = sem("projq"), sem("projkv")
        q_squared, kv_squared = sem("q_squared"), sem("kv_squared")
        q_rotated, kv_rotated, rope_added, k_ready = sem("q_rotated"), sem("kv_rotated"), sem("rope_added"), sem("k_ready")
        qk_tr, qk_hi, qk_lo = sem("qk_tr"), sem("qk_hi"), sem("qk_lo")
        scored, biased, exp_done, inverted = sem("scored"), sem("biased"), sem("exp_done"), sem("inverted")
        prob_ready, prob3_ready, norm_seed, norm_done, pool_own = (sem(n) for n in ("prob_ready", "prob3_ready", "norm_seed", "norm_done", "pool_own"))
        pt_tr, pt_hi, pt_lo, pv_step = sem("pt_tr"), sem("pt_hi"), sem("pt_lo"), sem("pv_step")
        at_hi, at_lo, o_done, o_added = sem("at_hi"), sem("at_lo"), sem("o_done"), sem("o_added")
        dve_own = sem("dve_own")
        FREE = {exp_done: 2, pt_lo: 2, pv_step: 4, at_lo: 1, o_added: 8, o_done: 5, projkv: 1, projq: 1, q_rotated: 1,
                q_squared: 1, kv_rotated: 1, kv_squared: 1, rope_added: 2, qk_lo: 1}
        block = ctx.enter_context(nc.Block())

        def wq(i, k):
            return w[i][:, k * CH:(k + 1) * CH]

        def wkv(i, k):
            return w[i][:, G * CH + k * 2 * HD:G * CH + (k + 1) * 2 * HD]

        def wo(i, h):
            return w[i][:, (QKV + h) * CH:(QKV + h + 1) * CH]

        def batches(engine, attend):
            attend(0, 0, True, False)
            with engine.Fori(0, HKV - 1) as g:
                for b in range(1, B):
                    attend(g, b, False, False)
                attend(g + 1, 0, False, False)
            for b in range(1, B):
                attend(HKV - 1, b, False, b == B - 1)

        def fill(h, place, handlers, first, last):
            for kind, i in FILL.get((h, place), ()):
                if kind in handlers and not (first and kind == "o") and not (last and kind not in "ou"):
                    handlers[kind](i)

        @block.sync
        def _(sp):
            def load(g, c, slot):
                src = wqkvo[g, c, :, :] if isinstance(g, int) else wqkvo[bass.ds(g, 1), c, :, :].rearrange("g p n -> (g p) n")
                sp.dma_start(stage[slot][:, :], src).then_inc(stage_in[slot], 16)

            def load_group(g, chunks):
                for i in chunks:
                    sp.wait_ge(w_split, NCH * g + QKV + i - RING + 1)
                    load(g if i < NCH - QKV else g + 1, (QKV + i) % NCH, (QKV + i) % RING)

            for i in range(RING):
                sp.sem_inc(stage_in[i], 16)
            for c in range(RING, QKV):
                sp.wait_ge(w_split, c - RING + 1)
                load(0, c, c % RING)
            with sp.Fori(0, HKV - 1) as g:
                load_group(g, range(NCH))
            load_group(HKV - 1, range(NCH - QKV))
            sp.wait_ge(w_split, NCH * HKV)

        @block.gpsimd
        def _(pool):
            def add_rope(j, t):
                pool.wait_ge(kv_rotated, FREE[kv_rotated] + TT * j + t + 1)
                nc.gpsimd.tensor_tensor(r[:, t, :], r[:, t, :], rot[t % 2][:, :], ALU.add).then_inc(rope_added, 1)

            def split_lo(s, c):
                pool.wait_ge(w_hi, s + 1)
                sl = slice(c * CH, (c + 1) * CH)
                nc.gpsimd.tensor_tensor(w[1][:, sl], stage[c % RING][:, :], w[0][:, sl].bitcast(F32),
                                        ALU.subtract).then_inc(w_split, 1)

            def newton(j):
                own = Steps(pool, pool_own, 1 + NEWTON_STEPS * j)
                y, half = rn[:, :, :].rearrange("p t h -> p (t h)"), ssum[:, :, :].rearrange("p t h -> p (t h)")
                pool.wait_ge(norm_seed, j + 1)
                for i in range(3):
                    own.chain(nc.gpsimd.tensor_tensor(n1[:, :], y, y, ALU.mult))
                    own.chain(nc.gpsimd.tensor_tensor(n2[:, :], n1[:, :], half, ALU.mult))
                    own.chain(nc.gpsimd.tensor_tensor(n1[:, :], n15[:, :], n2[:, :], ALU.subtract))
                    if i < 2:
                        own.chain(nc.gpsimd.tensor_tensor(y, y, n1[:, :], ALU.mult))
                nc.gpsimd.tensor_tensor(y, y, n1[:, :], ALU.mult).then_inc(norm_done, 1)
                assert own.n == NEWTON_STEPS

            def normalise(it, h, q):
                pool.wait_ge(inverted, 16 * it + 4 * h + q + 1)
                p = prob[h % 2][:, P_AT[q]:P_AT[q] + KEYS[q]]
                nc.gpsimd.tensor_tensor(p, p, rtotal[:, 4 * h + q:4 * h + q + 1].broadcast_to([P, KEYS[q]]), ALU.mult).then_inc(prob_ready, 1)

            def attend(g, b, first, last):
                it = 4 * g + b
                work = {"kv": lambda t: add_rope(it + 1, t), "n": lambda _: newton(it + 1)}
                for h in range(G):
                    normalise(it, h, 0)
                    normalise(it, h, 1)
                    fill(h, 1, work, first, last)
                    normalise(it, h, 2)
                    fill(h, 2, work, first, last)
                    fill(h, 3, work, first, last)
                if b == 0:
                    for c in range(QKV, NCH):
                        split_lo(NCH * g + c, c)
                if b == 2 and not (isinstance(g, int) and g == HKV - 1):
                    for c in range(QKV):
                        split_lo(NCH * (g + 1) + c, c)

            pool.sem_inc(rope_added, FREE[rope_added])
            for c in range(QKV):
                split_lo(c, c)
            nc.gpsimd.memset(n15[:, :], 1.5).then_inc(pool_own, 1)
            for t in range(TT):
                add_rope(0, t)
            newton(0)
            batches(pool, attend)

        @block.tensor
        def _(pe):
            def project(g, b, t, kv):
                j = 4 * g + b
                if t == 0 and not kv:
                    pe.wait_ge(ht_in, 16 * (j + 1))
                if b == 0 and t == 0:
                    pe.wait_ge(w_split, NCH * g + (QKV if kv else G))
                if kv:
                    pe.wait_ge(kv_rotated, FREE[kv_rotated] + TT * j + t)
                else:
                    pe.wait_ge(q_rotated, FREE[q_rotated] + TT * j + t)
                if t == 0:
                    pe.wait_ge(o_added, TT * j)
                o = bank[1][:, 0:2 * HD] if kv else bank[0][:, :]
                for k in range(KC):
                    for n, (a, c) in enumerate(SPLITS):
                        last = nc.tensor.matmul(o, hT[:, a, k, t * P:(t + 1) * P], wkv(c, k) if kv else wq(c, k),
                                                start=(k == 0 and n == 0), stop=(k == KC - 1 and n == 2))
                last.then_inc(projkv if kv else projq, 1)

            def transpose_qk(j, i):
                if i == 0:
                    pe.wait_ge(k_ready, j + 1)
                if i >= 2:
                    pe.wait_ge(qk_lo, FREE[qk_lo] + (G + 1) * j + {2: 0, 3: 1, 4: 3}[i])
                at = G * HD if i == 0 else (i - 1) * HD
                for t in range(TT):
                    last = nc.tensor.transpose(bank[TR[i]][:, t * P:(t + 1) * P], r[:, t, at:at + HD], ident[:, :])
                last.then_inc(qk_tr, 1)

            def score(it, b, h, q):
                if q == 0:
                    pe.wait_ge(qk_lo, FREE[qk_lo] + (G + 1) * it + h + 2)
                pe.wait_ge(exp_done, FREE[exp_done] + 16 * it + 4 * h + q - 1)
                o = bank[SC + q % 2]
                for n, (a, c) in enumerate(SPLITS):
                    nc.tensor.matmul(o[:, 0:KEYS[q]], qT[a][:, h, q * P:(q + 1) * P], kT[b % 2][c][:, 0:KEYS[q]], start=(n == 0), stop=False)
                nc.tensor.matmul(o[:, q * P:(q + 1) * P], identb[:, :], mask[:, :], start=False, stop=True).then_inc(scored, 1)

            def transpose_p(s, h, j):
                if j == 0:
                    pe.wait_ge(prob_ready, 3 * s + 3)
                    pe.wait_ge(prob3_ready, s + 1)
                pe.wait_ge(pt_lo, FREE[pt_lo] + 4 * s + j - 1)
                for q in range(j, TT):
                    last = nc.tensor.transpose(bank[PT + j % 2][:, (q - j) * P:(q - j + 1) * P],
                                               prob[h % 2][:, P_AT[q] + j * P:P_AT[q] + (j + 1) * P], ident[:, :])
                last.then_inc(pt_tr, 1)

            def values(s, b, h, j):
                if h == 0 and j == 0:
                    pe.wait_ge(kv_rotated, FREE[kv_rotated] + s + TT)
                if j == 0:
                    pe.wait_ge(at_lo, FREE[at_lo] + s)
                pe.wait_ge(pt_lo, FREE[pt_lo] + 4 * s + j + 1)
                for n, (a, c) in enumerate(SPLITS):
                    last = nc.tensor.matmul(bank[PV][:, j * P:S], v[b % 2][a][:, j, :], pT[c][:, PT_AT[j]:PT_AT[j] + QS[j]],
                                            start=(j == 0 and n == 0), stop=(j == TT - 1 and n == 2))
                last.then_inc(pv_step, 1)

            def output(g, b, t, projected):
                o = 4 * g + b
                if t == 0:
                    pe.wait_ge(w_split, NCH * (g + 1))
                    pe.wait_ge(at_lo, FREE[at_lo] + G * (o + 1))
                if projected and t == 0:
                    pe.wait_ge(q_rotated, FREE[q_rotated] + TT * (o + 2) + 4)
                if projected and t == 1:
                    pe.wait_ge(kv_rotated, FREE[kv_rotated] + TT * (o + 2) + 4)
                pe.wait_ge(o_added, FREE[o_added] + TT * o + max(t - 1, 0))
                for h in range(G):
                    for n, (a, c) in enumerate(SPLITS):
                        last = nc.tensor.matmul(bank[t % 2][:, :], aT[b % 2][a][:, h, t * P:(t + 1) * P], wo(c, h),
                                                start=(h == 0 and n == 0), stop=(h == G - 1 and n == 2))
                last.then_inc(o_done, 1)

            def attend(g, b, first, last):
                it = 4 * g + b
                gn, bn = (g, b + 1) if b < B - 1 else (g + 1, 0)
                gp, bp = (g, b - 1) if b else (g - 1, B - 1)
                work = {"q": lambda t: project(gn, bn, t, False), "kv": lambda t: project(gn, bn, t, True),
                        "o": lambda t: output(gp, bp, t, not last), "t": lambda i: transpose_qk(it + 1, i),
                        "u": lambda i: transpose_qk(it, i)}
                for h in range(G):
                    s, hp = G * it + h - 1, (h - 1) % G
                    bv = b if h else b - 1
                    before = not (first and h == 0)
                    score(it, b, h, 0)
                    score(it, b, h, 1)
                    fill(h, 1, work, first, last)
                    if h == int(first):
                        pe.wait_ge(qk_lo, FREE[qk_lo] + (G + 1) * it + G)
                    if before:
                        transpose_p(s, hp, 0)
                        transpose_p(s, hp, 1)
                    score(it, b, h, 2)
                    fill(h, 2, work, first, last)
                    if before:
                        values(s, bv, hp, 0)
                        transpose_p(s, hp, 2)
                        values(s, bv, hp, 1)
                        transpose_p(s, hp, 3)
                    score(it, b, h, 3)
                    if before:
                        values(s, bv, hp, 2)
                        values(s, bv, hp, 3)
                    fill(h, 3, work, first, last)

            pe.sem_inc(projkv, FREE[projkv])
            pe.sem_inc(projq, FREE[projq])
            pe.sem_inc(o_done, FREE[o_done])
            pe.sem_inc(pv_step, FREE[pv_step])
            for t in range(TT):
                project(0, 0, t, False)
                project(0, 0, t, True)
            for i in range(G):
                transpose_qk(0, i)
            batches(pe, attend)
            s = HQ * B - 1
            for j in range(TT):
                transpose_p(s, G - 1, j)
                if j:
                    values(s, B - 1, G - 1, j - 1)
            values(s, B - 1, G - 1, TT - 1)
            for t in range(TT):
                output(HKV - 1, B - 1, t, False)

        @block.scalar
        def _(act):
            def load_hT(j, bn):
                act.dma_start(hT[:, :, :, :].rearrange("p a k n -> p (a k n)").bitcast(F32), hT_dram[bn]).then_inc(ht_in, 16)

            def split_hi(s, c, nth):
                act.wait_ge(stage_in[c % RING], 16 * nth)
                nc.scalar.activation(w[0][:, c * CH:(c + 1) * CH], stage[c % RING][:, :], ACT.Copy).then_inc(w_hi, 1)

            def square_q(j, t):
                act.wait_ge(projq, FREE[projq] + TT * j + t + 1)
                act.wait_ge(rope_added, FREE[rope_added] + TT * j + t - 1)
                for h in range(G):
                    last = nc.scalar.activation(rot[t % 2][:, h * HD:(h + 1) * HD], bank[0][:, h * HD:(h + 1) * HD], ACT.Square,
                                                accum_out=ssum[:, t, h:h + 1])
                last.then_inc(q_squared, 1)

            def square_kv(j, b, t, more):
                act.wait_ge(projkv, FREE[projkv] + TT * j + t + 1)
                nc.scalar.activation(v[b % 2][0][:, t, :], bank[1][:, HD:2 * HD], ACT.Copy)
                nc.scalar.activation(rot[t % 2][:, G * HD:R], bank[1][:, 0:HD], ACT.Square, accum_out=ssum[:, t, G:G + 1]).then_inc(kv_squared, 1)
                if t == TT - 1 and more:
                    load_hT(j + 1, (b + 1) % B)

            def exponentials(it, b, h, q):
                act.wait_ge(biased, 16 * it + 4 * h + q + 1)
                nc.scalar.activation(prob[h % 2][:, P_AT[q]:P_AT[q] + KEYS[q]], bank[SC + q % 2][:, 0:KEYS[q]], ACT.Exp,
                                     bias=bias[:, 4 * h + q:4 * h + q + 1], scale=scale[b % 2][:, q, h:h + 1],
                                     accum_out=total[:, 4 * h + q:4 * h + q + 1]).then_inc(exp_done, 1)

            def hi_p(s, j):
                act.wait_ge(pt_tr, 4 * s + j + 1)
                act.wait_ge(pv_step, FREE[pv_step] + 4 * s + j - 3)
                nc.scalar.activation(pT[0][:, PT_AT[j]:PT_AT[j] + QS[j]], bank[PT + j % 2][:, 0:QS[j]], ACT.Copy).then_inc(pt_hi, 1)

            def hi_attn(s, b, h):
                act.wait_ge(pv_step, FREE[pv_step] + 4 * s + 4)
                if h == 0:
                    act.wait_ge(o_done, FREE[o_done] + s - TT)
                nc.scalar.activation(aT[b % 2][0][:, h, :], bank[PV][:, :], ACT.Copy).then_inc(at_hi, 1)

            def hi_qk(j, bn, i):
                act.wait_ge(qk_tr, (G + 1) * j + i + 1)
                o = kT[bn % 2][0][:, :] if i == 0 else qT[0][:, i - 1, :]
                nc.scalar.activation(o, bank[TR[i]][:, :], ACT.Copy).then_inc(qk_hi, 1)

            def attend(g, b, first, last):
                it, bn = 4 * g + b, (b + 1) % B
                final = isinstance(g, int) and g == HKV - 1
                work = {"q": lambda t: square_q(it + 1, t), "kv": lambda t: square_kv(it + 1, bn, t, not (final and b == 2)),
                        "t": lambda i: hi_qk(it + 1, bn, i), "u": lambda i: hi_qk(it, b, i)}
                for h in range(G):
                    s, hp = G * it + h - 1, (h - 1) % G
                    before = not (first and h == 0)
                    exponentials(it, b, h, 0)
                    exponentials(it, b, h, 1)
                    if before:
                        hi_p(s, 0)
                        hi_p(s, 1)
                    fill(h, 1, work, first, last)
                    exponentials(it, b, h, 2)
                    if before:
                        hi_p(s, 2)
                        hi_p(s, 3)
                    fill(h, 2, work, first, last)
                    exponentials(it, b, h, 3)
                    if before:
                        hi_attn(s, b if h else b - 1, hp)
                    fill(h, 3, work, first, last)
                if b == 0:
                    act.wait_ge(o_done, FREE[o_done] + 4 * TT * g)
                    for c in range(QKV, NCH):
                        split_hi(NCH * g + c, c, 2 * g + c // RING + 1)
                if b == 2 and not final:
                    act.wait_ge(projkv, FREE[projkv] + 4 * TT * (g + 1))
                    for c in range(QKV):
                        split_hi(NCH * (g + 1) + c, c, 2 * (g + 1) + c // RING + 1)

            for s in (exp_done, q_squared, kv_squared):
                act.sem_inc(s, FREE[s])
            load_hT(0, 0)
            for c in range(QKV):
                split_hi(c, c, c // RING + 1)
            for t in range(TT):
                square_q(0, t)
                square_kv(0, 0, t, True)
            for i in range(G):
                hi_qk(0, 0, i)
            batches(act, attend)
            for j in range(TT):
                hi_p(HQ * B - 1, j)
            hi_attn(HQ * B - 1, B - 1, G - 1)

        @block.vector
        def _(dve):
            def rotate(j, t, kv):
                n, at, heads, name = (bank[1][:, 0:HD], G * HD, 1, "k") if kv else (bank[0][:, :], 0, G, "q")
                src = n.rearrange("p (h d) -> p h d", h=heads)
                if kv:
                    dve.wait_ge(kv_squared, FREE[kv_squared] + TT * j + t + 1)
                else:
                    dve.wait_ge(q_squared, FREE[q_squared] + TT * j + t + 1)
                    dve.wait_ge(rope_added, FREE[rope_added] + TT * j + t - 1)
                o = r[:, t, at:at + heads * HD].rearrange("p (h d) -> p h d", h=heads)
                o2 = rot[t % 2][:, at:at + heads * HD].rearrange("p (h d) -> p h d", h=heads)
                H = HD // 2
                c, s = tab[name, "c"][:, t, :], tab[name, "s"][:, t, :]
                nc.vector.tensor_tensor(o, src, c.unsqueeze(1).broadcast_to([P, heads, HD]), ALU.mult)
                nc.vector.tensor_tensor(o2[:, :, 0:H], src[:, :, H:HD], s[:, 0:H].unsqueeze(1).broadcast_to([P, heads, H]), ALU.mult)
                last = nc.vector.tensor_tensor(o2[:, :, H:HD], src[:, :, 0:H], s[:, H:HD].unsqueeze(1).broadcast_to([P, heads, H]), ALU.mult)
                if not kv:
                    last.then_inc(q_rotated, 1)

            def rest_kv(j, b, t):
                rotate(j, t, True)
                nc.vector.tensor_tensor(v[b % 2][1][:, t, :], bank[1][:, HD:2 * HD], v[b % 2][0][:, t, :].bitcast(F32),
                                        ALU.subtract).then_inc(kv_rotated, 1)

            def start_norms(j, own):
                flat, u = ssum[:, :, :].rearrange("p t h -> p (t h)"), n1[:, :]
                own.chain(nc.vector.tensor_scalar(flat, flat, 0.5 / HD, 0.5e-6, ALU.mult, ALU.add))
                own.chain(nc.vector.tensor_scalar(u.bitcast(U32), flat.bitcast(U32), 1, None, ALU.logical_shift_right))
                nc.vector.tensor_scalar(rn[:, :, :].rearrange("p t h -> p (t h)").bitcast(I32), u.bitcast(I32), -1.0,
                                        RSQRT_MAGIC - 2.0 ** 22, ALU.mult, ALU.add).then_inc(norm_seed, 1)

            def apply_norms(j, b, own):
                dve.wait_ge(norm_done, j + 1)
                dve.wait_ge(rope_added, FREE[rope_added] + TT * (j + 1))
                k = r[:, :, G * HD:R]
                nc.vector.tensor_tensor(k, k, rn[:, :, G:G + 1].broadcast_to([P, TT, HD]), ALU.mult).then_inc(k_ready, 1)
                own.done(nc.vector.tensor_scalar(scale[b % 2][:, :, :], rn[:, :, 0:G], HD ** -0.5, None, ALU.mult))
                own.chain(nc.vector.tensor_scalar(nscale[b % 2][:, :, :], rn[:, :, 0:G], -HD ** -0.5, None, ALU.mult))

            def maxima(it, b, h, q, own):
                n = 4 * h + q
                dve.wait_ge(scored, 16 * it + n + 1)
                own.chain(nc.vector.tensor_reduce(top[:, n:n + 1], bank[SC + q % 2][:, 0:KEYS[q]], AX.X, ALU.max))
                nc.vector.tensor_tensor(bias[:, n:n + 1], top[:, n:n + 1], nscale[b % 2][:, q, h:h + 1], ALU.mult).then_inc(biased, 1)

            def invert(it, h, q):
                n = 4 * h + q
                dve.wait_ge(exp_done, FREE[exp_done] + 16 * it + n + 1)
                nc.vector.reciprocal(rtotal[:, n:n + 1], total[:, n:n + 1]).then_inc(inverted, 1)
                if q == TT - 1:
                    dve.wait_ge(inverted, 16 * it + n + 1)
                    p = prob[h % 2][:, P_AT[q]:P_AT[q] + KEYS[q]]
                    nc.vector.tensor_scalar(p, p, rtotal[:, n:n + 1], None, ALU.mult).then_inc(prob3_ready, 1)

            def lo_p(s, j):
                dve.wait_ge(pt_hi, 4 * s + j + 1)
                sl = slice(PT_AT[j], PT_AT[j] + QS[j])
                nc.vector.tensor_tensor(pT[1][:, sl], bank[PT + j % 2][:, 0:QS[j]], pT[0][:, sl].bitcast(F32), ALU.subtract).then_inc(pt_lo, 1)

            def lo_attn(s, b, h):
                dve.wait_ge(at_hi, s + 1)
                nc.vector.tensor_tensor(aT[b % 2][1][:, h, :], bank[PV][:, :], aT[b % 2][0][:, h, :].bitcast(F32), ALU.subtract).then_inc(at_lo, 1)

            def lo_qk(j, bn, i):
                dve.wait_ge(qk_hi, (G + 1) * j + i + 1)
                hi, lo = (kT[bn % 2][0][:, :], kT[bn % 2][1][:, :]) if i == 0 else (qT[0][:, i - 1, :], qT[1][:, i - 1, :])
                nc.vector.tensor_tensor(lo, bank[TR[i]][:, :], hi.bitcast(F32), ALU.subtract).then_inc(qk_lo, 1)

            def add_output(o, b, t):
                dve.wait_ge(o_done, FREE[o_done] + TT * o + t + 1)
                a = acc[:, b * TT + t, :]
                nc.vector.tensor_tensor(a, bank[t % 2][:, :], a, ALU.add).then_inc(o_added, 1)

            def attend(g, b, first, last):
                it, bn = 4 * g + b, (b + 1) % B
                own = Steps(dve, dve_own, NORM_STEPS + (NORM_STEPS + 4 * G) * it)
                work = {"q": lambda t: rotate(it + 1, t, False), "kv": lambda t: rest_kv(it + 1, bn, t),
                        "o": lambda t: add_output(it - 1, (b - 1) % B, t), "t": lambda i: lo_qk(it + 1, bn, i),
                        "u": lambda i: lo_qk(it, b, i), "n": lambda _: start_norms(it + 1, own), "m": lambda _: apply_norms(it + 1, bn, own)}
                for h in range(G):
                    s, hp = G * it + h - 1, (h - 1) % G
                    before = not (first and h == 0)
                    maxima(it, b, h, 0, own)
                    maxima(it, b, h, 1, own)
                    invert(it, h, 0)
                    invert(it, h, 1)
                    if before:
                        lo_p(s, 0)
                        lo_p(s, 1)
                    maxima(it, b, h, 2, own)
                    fill(h, 1, work, first, last)
                    invert(it, h, 2)
                    if before:
                        lo_p(s, 2)
                        lo_p(s, 3)
                    maxima(it, b, h, 3, own)
                    fill(h, 2, work, first, last)
                    invert(it, h, 3)
                    if before:
                        lo_attn(s, b if h else b - 1, hp)
                    fill(h, 3, work, first, last)
                assert own.n == 4 * G + (0 if last else NORM_STEPS), own.n

            for s in (pt_lo, at_lo, o_added, q_rotated, kv_rotated, qk_lo):
                dve.sem_inc(s, FREE[s])
            for t in range(TT):
                rotate(0, t, False)
                rest_kv(0, 0, t)
            norms0 = Steps(dve, dve_own)
            start_norms(0, norms0)
            apply_norms(0, 0, norms0)
            assert norms0.n == NORM_STEPS, norms0.n
            for i in range(G):
                lo_qk(0, 0, i)
            batches(dve, attend)
            s = HQ * B - 1
            for j in range(TT):
                lo_p(s, j)
            lo_attn(s, B - 1, G - 1)
            for t in range(TT):
                add_output(HKV * B - 1, B - 1, t)


NORM_STEPS = 4
NEWTON_STEPS = 11


def router(nc, w_ffn, gateT, ranklow_d, acc, ident, tokT, combine, x1_dram):
    with ExitStack() as ctx:
        def sb(name, shape, dt=F32):
            return ctx.enter_context(nc.sbuf_tensor(name, shape, dt))

        def sem(name):
            return ctx.enter_context(nc.semaphore(name))

        x1 = sb("x1", [P, NT, D])
        wcol = sb("wcol2", [P, KC])
        gate = sb("gate", [P, KC, P])
        gs = [sb(f"gate_{n}", [P, KC, P], F32R) for n in ("hi", "lo")]
        low = sb("low", [P, E, E])
        junk = sb("junk", [P, D])
        ms = sb("ms", [P, TT])
        rms, t1, t2 = sb("rms", [P, TT]), sb("rt1", [P, TT]), sb("rt2", [P, TT])
        hn = sb("hn2", [P, TT, D])
        lt = sb("lt", [P, S])
        logits = sb("logits", [P, NT, E])
        top, den = sb("rtop", [P, NT]), sb("den", [P, NT])
        prob, chosen, rank = sb("rprob", [P, NT, E]), sb("chosen", [P, NT, E]), sb("rank", [P, NT, E])
        above, tied = sb("above", [P, NT, E, E]), sb("tied", [P, NT, E, E])
        tr = [ctx.enter_context(nc.psum_tensor(f"tr{i}", [P, S], F32)) for i in range(2)]
        pl = ctx.enter_context(nc.psum_tensor("pl", [P, S], F32))
        plt = ctx.enter_context(nc.psum_tensor("plt", [P, TT, P], F32))
        const_in, x1_in = sem("rconst_in"), sem("x1_in")
        squares, hn_ready, tr_done, tok_hi, tok_lo = sem("squares"), sem("rhn_ready"), sem("rtr_done"), sem("tok_hi"), sem("tok_lo")
        gate_split, logit_done, lt_ready, lt_tr, logit_ready = (sem(n) for n in ("gate_split", "logit_done", "lt_ready", "lt_tr", "logit_ready"))
        shifted, exped, x1_added, own_sem = sem("shifted"), sem("exped"), sem("x1_added"), sem("rown")
        block = ctx.enter_context(nc.Block())

        @block.sync
        def _(sp):
            sp.dma_start(wcol[:, :], w_ffn).then_inc(const_in, 16)
            sp.dma_start(gate[:, :, :], gateT.rearrange("c p e -> p c e")).then_inc(const_in, 16)
            sp.dma_start(low[:, :, :].rearrange("p a b -> p (a b)"), ranklow_d.broadcast_to([P, E * E])).then_inc(const_in, 16)
            sp.dma_start(x1[:, :, :], x1_dram).then_inc(x1_in, 16)

        @block.gpsimd
        def _(pool):
            pool.wait_ge(x1_in, 16)
            with pool.Fori(0, B) as b:
                pool.wait_ge(hn_ready, TT * (b + 1))
                a = acc[:, bass.ds(b * TT, TT), :].rearrange("p t d -> p (t d)")
                nc.gpsimd.tensor_tensor(a, a, x1[:, bass.ds(b * TT, TT), :].rearrange("p t d -> p (t d)"), ALU.add).then_inc(x1_added, 1)
            pool.wait_ge(x1_added, B)

        @block.scalar
        def _(act):
            act.wait_ge(const_in, 48)
            with act.Fori(0, B) as b:
                for t in range(TT):
                    last = nc.scalar.activation(junk[:, :], acc[:, bass.ds(b * TT + t, 1), :].rearrange("p a d -> p (a d)"), ACT.Square,
                                                accum_out=ms[:, t:t + 1])
                    last.then_inc(squares, 1)
                    act.wait_ge(squares, TT * b + t + 1)
                for t in range(TT):
                    act.wait_ge(tr_done, TT * b + t + 1)
                    for k in range(KC):
                        last = nc.scalar.activation(tokT[0][:, k, bass.ds(b * S + t * P, P)], tr[t % 2][:, k * P:(k + 1) * P], ACT.Copy,
                                                    scale=wcol[:, k:k + 1])
                    last.then_inc(tok_hi, 1)
                act.wait_ge(logit_done, b + 1)
                nc.scalar.activation(lt[:, :], pl[:, :], ACT.Copy).then_inc(lt_ready, 1)
            act.wait_ge(shifted, 1)
            nc.scalar.activation(prob[:, :, :], logits[:, :, :], ACT.Exp).then_inc(exped, 1)

        @block.tensor
        def _(pe):
            pe.wait_ge(gate_split, 2)
            with pe.Fori(0, B) as b:
                for t in range(TT):
                    pe.wait_ge(hn_ready, TT * b + t + 1)
                    if t >= 2:
                        pe.wait_ge(tok_lo, TT * b + t - 1)
                    for k in range(KC):
                        last = nc.tensor.transpose(tr[t % 2][:, k * P:(k + 1) * P], hn[:, t, k * P:(k + 1) * P], ident[:, :])
                    last.then_inc(tr_done, 1)
                pe.wait_ge(tok_lo, TT * (b + 1))
                for k in range(KC):
                    for n, (a, c) in enumerate(SPLITS):
                        last = nc.tensor.matmul(pl[:, :], gs[a][:, k, :], tokT[c][:, k, bass.ds(b * S, S)],
                                                start=(k == 0 and n == 0), stop=(k == KC - 1 and n == 2))
                last.then_inc(logit_done, 1)
                pe.wait_ge(lt_ready, b + 1)
                for t in range(TT):
                    last = nc.tensor.transpose(plt[:, t, :], lt[:, t * P:(t + 1) * P], ident[:, :])
                last.then_inc(lt_tr, 1)

        @block.vector
        def _(dve):
            pre = Steps(dve, own_sem)
            dve.wait_ge(const_in, 48)
            nc.vector.tensor_copy(gs[0][:, :, :], gate[:, :, :]).then_inc(gate_split, 1)
            dve.wait_ge(gate_split, 1)
            nc.vector.tensor_tensor(gs[1][:, :, :], gate[:, :, :], gs[0][:, :, :].bitcast(F32), ALU.subtract).then_inc(gate_split, 1)
            with dve.Fori(0, B) as b:
                own = Steps(dve, own_sem, pre.n + b * ROUTER_STEPS)
                dve.wait_ge(squares, TT * (b + 1))
                own.chain(nc.vector.tensor_scalar(ms[:, :], ms[:, :], 1.0 / D, 1e-6, ALU.mult, ALU.add))
                rsqrt(nc, own.chain, rms[:, :], ms[:, :], t1[:, :], t2[:, :])
                for t in range(TT):
                    nc.vector.tensor_scalar(hn[:, t, :], acc[:, bass.ds(b * TT + t, 1), :].rearrange("p a d -> p (a d)"), rms[:, t:t + 1],
                                            None, ALU.mult).then_inc(hn_ready, 1)
                for t in range(TT):
                    dve.wait_ge(tok_hi, TT * b + t + 1)
                    for k in range(KC):
                        last = nc.vector.scalar_tensor_tensor(tokT[1][:, k, bass.ds(b * S + t * P, P)], tr[t % 2][:, k * P:(k + 1) * P],
                                                              wcol[:, k:k + 1], tokT[0][:, k, bass.ds(b * S + t * P, P)].bitcast(F32),
                                                              ALU.mult, ALU.subtract)
                    last.then_inc(tok_lo, 1)
                dve.wait_ge(lt_tr, b + 1)
                nc.vector.tensor_copy(logits[:, bass.ds(b * TT, TT), :], plt[:, :, 0:E]).then_inc(logit_ready, 1)
                assert own.n == ROUTER_STEPS, own.n
            dve.wait_ge(logit_ready, B)
            end = Steps(dve, own_sem, pre.n + B * ROUTER_STEPS)
            row = [P, NT, E]
            end.chain(nc.vector.tensor_reduce(top[:, :], logits[:, :, :], AX.X, ALU.max))
            nc.vector.tensor_tensor(logits[:, :, :], logits[:, :, :], top[:, :].unsqueeze(2).broadcast_to(row), ALU.subtract).then_inc(shifted, 1)
            dve.wait_ge(exped, 1)
            end.chain(nc.vector.tensor_reduce(den[:, :], prob[:, :, :], AX.X, ALU.add))
            end.chain(nc.vector.reciprocal(top[:, :], den[:, :]))
            end.chain(nc.vector.tensor_tensor(prob[:, :, :], prob[:, :, :], top[:, :].unsqueeze(2).broadcast_to(row), ALU.mult))
            pair = [P, NT, E, E]
            other, mine = prob[:, :, :].unsqueeze(2).broadcast_to(pair), prob[:, :, :].unsqueeze(3).broadcast_to(pair)
            end.done(nc.vector.tensor_tensor(above[:, :, :, :], other, mine, ALU.is_gt))
            end.chain(nc.vector.tensor_tensor(tied[:, :, :, :], other, mine, ALU.is_equal))
            end.chain(nc.vector.tensor_tensor(tied[:, :, :, :], tied[:, :, :, :], low[:, :, :].unsqueeze(1).broadcast_to(pair), ALU.mult))
            end.chain(nc.vector.tensor_tensor(above[:, :, :, :], above[:, :, :, :], tied[:, :, :, :], ALU.add))
            end.chain(nc.vector.tensor_reduce(rank[:, :, :], above[:, :, :, :], AX.X, ALU.add))
            end.chain(nc.vector.tensor_scalar(chosen[:, :, :], rank[:, :, :], 1.5, None, ALU.is_lt))
            end.chain(nc.vector.tensor_tensor(chosen[:, :, :], chosen[:, :, :], prob[:, :, :], ALU.mult))
            end.chain(nc.vector.tensor_reduce(den[:, :], chosen[:, :, :], AX.X, ALU.add))
            end.chain(nc.vector.tensor_scalar(den[:, :], den[:, :], 1e-9, None, ALU.add))
            end.chain(nc.vector.reciprocal(top[:, :], den[:, :]))
            end.chain(nc.vector.tensor_tensor(combine[:, :, :], chosen[:, :, :], top[:, :].unsqueeze(2).broadcast_to(row), ALU.mult))


ROUTER_STEPS = 12
CW = 768
NCW = 6


def experts(nc, wexp, acc, tokT, combine, out):
    with ExitStack() as ctx:
        def sb(name, shape, dt=F32):
            return ctx.enter_context(nc.sbuf_tensor(name, shape, dt))

        def sem(name):
            return ctx.enter_context(nc.semaphore(name))

        stage = [sb(f"wstage{i}", [P, CW]) for i in range(2)]
        w = [[sb(f"we{i}_{n}", [P, NCW * CW], F32R) for n in ("hi", "lo")] for i in range(2)]
        gated = [sb(f"gated{i}", [P, S]) for i in range(2)]
        h = [[sb(f"h{i}_{n}", [P, IC, S], F32R) for n in ("hi", "lo")] for i in range(2)]
        bank = [ctx.enter_context(nc.psum_tensor(f"ebank{i}", [P, S], F32)) for i in range(8)]
        DOWN = 4
        stage_in = [sem(f"wstage_in{i}") for i in range(2)]
        passed = sem("passed3")
        w_hi, w_split, up_done, silu_done, gate_done = sem("we_hi"), sem("we_split"), sem("up_done"), sem("silu_done"), sem("gate_done")
        h_hi, h_lo, down_done, added, stored = sem("h_hi"), sem("h_lo"), sem("down_done"), sem("added"), sem("stored")
        FREE = {w_split: 2, gate_done: 2, h_lo: 2, down_done: 17, added: 4}
        STEPS = 2 * B
        block = ctx.enter_context(nc.Block())

        def wgu(eh, part, up, k, c):
            at = up * KC * IP + k * IP + c * P
            return w[eh][part][:, at:at + P]

        def wdown(eh, part, c):
            at = 2 * KC * IP + c * D
            return w[eh][part][:, at:at + D]

        @block.sync
        def _(sp):
            with sp.Fori(0, E // 2) as g:
                for i in range(2 * NCW):
                    sp.wait_ge(w_split, FREE[w_split] + 2 * NCW * g + i - 1)
                    sp.dma_start(stage[i % 2][:, :], wexp[bass.ds(2 * g + i // NCW, 1), i % NCW, :, :].rearrange("g p n -> (g p) n")
                                 ).then_inc(stage_in[i % 2], 16)
            for b in range(B):
                sp.wait_ge(added, FREE[added] + TT * ((E - 1) * B + b + 1))
                sp.dma_start(out[b * S:(b + 1) * S, :].rearrange("(t p) d -> p t d", p=P), acc[:, b * TT:(b + 1) * TT, :]).then_inc(stored, 16)
            sp.wait_ge(stored, 16 * B)

        @block.gpsimd
        def _(pool):
            with pool.Fori(0, E // 2) as g:
                for i in range(2 * NCW):
                    eh, c = i // NCW, i % NCW
                    if c == 0:
                        pool.wait_ge(down_done, FREE[down_done] + 16 * (2 * g + eh) - 16)
                    wait_apart(pool, passed, stage_in[i % 2], 16 * (NCW * g + i // 2 + 1))
                    sl = slice(c * CW, (c + 1) * CW)
                    nc.gpsimd.tensor_copy(w[eh][0][:, sl], stage[i % 2][:, :]).then_inc(w_hi, 1)
                    pool.wait_ge(w_hi, 2 * NCW * g + i + 1)
                    nc.gpsimd.tensor_tensor(w[eh][1][:, sl], stage[i % 2][:, :], w[eh][0][:, sl].bitcast(F32), ALU.subtract).then_inc(w_split, 1)

        @block.tensor
        def _(pe):
            def up(g, n, c):
                eh, b = n // B, n % B
                k0 = IC * n + c
                if b == 0 and c == 0:
                    pe.wait_ge(w_split, FREE[w_split] + NCW * (2 * g + eh + 1))
                pe.wait_ge(gate_done, FREE[gate_done] + IC * STEPS * g + k0 - 1)
                for u in range(2):
                    for k in range(KC):
                        for i, (a, m) in enumerate(SPLITS):
                            last = nc.tensor.matmul(bank[2 * (k0 % 2) + u][:, :], wgu(eh, a, u, k, c), tokT[m][:, k, b * S:(b + 1) * S],
                                                    start=(k == 0 and i == 0), stop=(k == KC - 1 and i == 2))
                last.then_inc(up_done, 1)

            def down(g, n, t):
                eh = n // B
                if t == 0:
                    pe.wait_ge(h_lo, FREE[h_lo] + IC * (STEPS * g + n + 1))
                pe.wait_ge(added, FREE[added] + TT * (STEPS * g + n) + t - 3)
                for c in range(IC):
                    for i, (a, m) in enumerate(SPLITS):
                        last = nc.tensor.matmul(bank[DOWN + t][:, :], h[n % 2][a][:, c, t * P:(t + 1) * P], wdown(eh, m, c),
                                                start=(c == 0 and i == 0), stop=(c == IC - 1 and i == 2))
                last.then_inc(down_done, 1)

            pe.sem_inc(down_done, FREE[down_done])
            with pe.Fori(0, E // 2) as g:
                for n in range(STEPS):
                    for c, downs in enumerate(((0,), (1, 2), (3,))):
                        up(g, n, c)
                        if n:
                            for t in downs:
                                down(g, n - 1, t)
                for t in range(TT):
                    down(g, STEPS - 1, t)

        @block.scalar
        def _(act):
            with act.Fori(0, E // 2) as g:
                for n in range(STEPS):
                    for c in range(IC):
                        k0 = IC * n + c
                        act.wait_ge(up_done, IC * STEPS * g + k0 + 1)
                        act.wait_ge(h_lo, FREE[h_lo] + IC * STEPS * g + k0 - 1)
                        nc.scalar.activation(gated[k0 % 2][:, :], bank[2 * (k0 % 2)][:, :], ACT.Silu).then_inc(silu_done, 1)
                        act.wait_ge(gate_done, FREE[gate_done] + IC * STEPS * g + k0 + 1)
                        if c == 0:
                            act.wait_ge(down_done, FREE[down_done] + TT * (STEPS * g + n) - TT)
                        nc.scalar.activation(h[n % 2][0][:, c, :], gated[k0 % 2][:, :], ACT.Copy).then_inc(h_hi, 1)

        @block.vector
        def _(dve):
            def add(g, n, t):
                tile = (n % B) * TT + t
                dve.wait_ge(down_done, FREE[down_done] + TT * (STEPS * g + n) + t + 1)
                nc.vector.scalar_tensor_tensor(acc[:, tile, :], bank[DOWN + t][:, :],
                                               combine[:, tile, bass.ds(2 * g + n // B, 1)], acc[:, tile, :],
                                               ALU.mult, ALU.add).then_inc(added, 1)

            for s in (w_split, gate_done, h_lo, added):
                dve.sem_inc(s, FREE[s])
            with dve.Fori(0, E // 2) as g:
                for n in range(STEPS):
                    for c, downs in enumerate(((0,), (1, 2), (3,))):
                        k0 = IC * n + c
                        o = gated[k0 % 2]
                        dve.wait_ge(silu_done, IC * STEPS * g + k0 + 1)
                        nc.vector.tensor_tensor(o[:, :], bank[2 * (k0 % 2) + 1][:, :], o[:, :], ALU.mult).then_inc(gate_done, 1)
                        dve.wait_ge(h_hi, IC * STEPS * g + k0 + 1)
                        nc.vector.tensor_tensor(h[n % 2][1][:, c, :], o[:, :], h[n % 2][0][:, c, :].bitcast(F32), ALU.subtract).then_inc(h_lo, 1)
                        if n:
                            for t in downs:
                                add(g, n - 1, t)
                for t in range(TT):
                    add(g, STEPS - 1, t)


def kernel(x, ctx_2048, L0_ffn_attn_norm_w, L0_ffn_q_w, L0_ffn_k_w, L0_ffn_v_w, L0_ffn_o_w, L0_ffn_q_norm_w, L0_ffn_k_norm_w,
           L0_ffn_ffn_norm_w, L0_ffn_gate_w, L0_ffn_wg, L0_ffn_wu, L0_ffn_wd):
    import numpy as np
    import concourse.bacc as bacc
    from concourse.bass_utils import run_bass_kernel_spmd

    f = np.float32
    qT = np.asarray(L0_ffn_q_w).reshape(HKV, G * HD, D).transpose(0, 2, 1)
    kT = np.asarray(L0_ffn_k_w).reshape(HKV, HD, D).transpose(0, 2, 1)
    vT = np.asarray(L0_ffn_v_w).reshape(HKV, HD, D).transpose(0, 2, 1)
    oT = np.asarray(L0_ffn_o_w).T.reshape(HKV, G, HD, D)
    wqkvo = np.zeros((HKV, 10, P, 512), f)
    wqkvo[:, 0:4] = qT.reshape(HKV, KC, P, 512)
    kv = np.concatenate([kT, vT], axis=2).reshape(HKV, 2, 2, P, 2 * HD)
    wqkvo[:, 4:6] = kv.transpose(0, 1, 3, 2, 4).reshape(HKV, 2, P, 512)
    wqkvo[:, 6:10] = oT
    wexp = np.zeros((E, NCW, P, CW), f)
    for n, a in enumerate((L0_ffn_wg, L0_ffn_wu)):
        padded = np.zeros((E, D, IP), f)
        padded[:, :, :I] = np.asarray(a).transpose(0, 2, 1)
        padded = padded.reshape(E, KC, P, IP).transpose(0, 2, 1, 3).reshape(E, P, 2, CW)
        wexp[:, 2 * n:2 * n + 2] = padded.transpose(0, 2, 1, 3)
    padded = np.zeros((E, IP, D), f)
    padded[:, :I] = np.asarray(L0_ffn_wd).transpose(0, 2, 1)
    padded = padded.reshape(E, IC, P, D).transpose(0, 2, 1, 3).reshape(E, P, 2, CW)
    wexp[:, 4:6] = padded.transpose(0, 2, 1, 3)
    gateT = np.zeros((KC, P, P), f)
    gateT[:, :, :E] = np.asarray(L0_ffn_gate_w).T.reshape(KC, P, E)
    freqs = (f(1.0) / np.power(f(1000000.0), np.arange(0, HD, 2, dtype=f) / f(HD), dtype=f)).astype(f)
    angle = np.outer(np.arange(S, dtype=f), freqs).astype(f)
    tables = [t.astype(f).reshape(TT, P, HD // 2).transpose(1, 0, 2).reshape(P, TT * HD // 2) for t in (np.cos(angle), np.sin(angle))]
    mask = np.where(np.arange(P)[None, :] > np.arange(P)[:, None], f(-1e30), f(0.0)).astype(f)
    low = (np.arange(E)[None, :] < np.arange(E)[:, None]).astype(f).reshape(1, E * E)
    arrays = {
        "x": np.asarray(x).reshape(B * S, D), "ctxT": np.asarray(ctx_2048).transpose(0, 2, 1), "w_attn": np.asarray(L0_ffn_attn_norm_w).reshape(KC, P).T,
        "wqkvo": wqkvo, "qn": np.asarray(L0_ffn_q_norm_w), "kn": np.asarray(L0_ffn_k_norm_w), "cos": tables[0], "sin": tables[1],
        "w_ffn": np.asarray(L0_ffn_ffn_norm_w).reshape(KC, P).T, "gateT": gateT, "wexp": wexp, "ident": np.eye(P, dtype=f), "mask": mask, "ranklow": low,
    }
    arrays = {f"in_{n}": np.ascontiguousarray(a) for n, a in arrays.items()}
    nc = bacc.Bacc("TRN2", target_bir_lowering=False, num_devices=1)
    args = [nc.dram_tensor(n, a.shape, mybir.dt.from_np(a.dtype), kind="ExternalInput").ap() for n, a in arrays.items()]
    out = nc.dram_tensor("out", (B * S, D), F32, kind="ExternalOutput").ap()
    build(nc, *args, out)
    r = run_bass_kernel_spmd(nc, [arrays], core_ids=[0])
    return r.results[0]["out"].reshape(B, S, D)
```
